# Optimizing a Trainium2 kernel written in Bass

```python
import numpy as np
import jax
import jax.numpy as jnp

def _softmax(x, axis=-1):
    return jax.nn.softmax(x, axis=axis)

def _gelu(x):
    return jax.nn.gelu(x, approximate=True)

def _silu(x):
    return jax.nn.silu(x)

def _sigmoid(x):
    return jax.nn.sigmoid(x)

def _layernorm(x, axis=-1, eps=1e-05):
    m = jnp.mean(x, axis=axis, keepdims=True)
    v = jnp.var(x, axis=axis, keepdims=True)
    return (x - m) / jnp.sqrt(v + eps)

def _scatter_add(tgt, idx, src, axis=0):
    return tgt.at[idx].add(src)

def _segment_sum(src, seg, n):
    return jax.ops.segment_sum(src, seg, n)
kernel_name = 'mk_seq_postln_d1_jaxref_r8_165bb6'

def setup_inputs(seed: int=0):
    np.random.seed(seed)
    _w = jnp.asarray

    def _L0_attn_setup():
        import jax, jax.numpy as jnp
        import numpy as np
        EPS = 1e-06

        def _l2_norm(t):
            inv = 1.0 / jnp.linalg.norm(t, ord=2, axis=-2)
            return t * inv[:, None, :]
        key = jax.random.key(seed)
        ks = jax.random.split(key, 8)
        B, C, D = (16, 256, 128)
        s = 1.0 / np.sqrt(D)
        return {'x': jax.random.normal(ks[0], (B, C, D), dtype=jnp.float32), 'Wq': jax.random.normal(ks[1], (D, D), dtype=jnp.float32) * s, 'bq': jnp.zeros((D,), dtype=jnp.float32), 'Wk': jax.random.normal(ks[2], (D, D), dtype=jnp.float32) * s, 'bk': jnp.zeros((D,), dtype=jnp.float32), 'Wv': jax.random.normal(ks[3], (D, D), dtype=jnp.float32) * s, 'bv': jnp.zeros((D,), dtype=jnp.float32), 'gamma': jax.random.normal(ks[4], (1,), dtype=jnp.float32) * 0.1}
    _L0_attn_in = _L0_attn_setup()

    def _L0_ffn_setup():
        import jax, jax.numpy as jnp
        import numpy as np
        N_EMBD = 128
        NUM_EXPERTS = 8
        TOP_K = 2

        def new_gelu(x):
            c = jnp.sqrt(2.0 / jnp.pi).astype(x.dtype)
            return 0.5 * x * (1.0 + jnp.tanh(c * (x + 0.044715 * x ** 3)))
        key = jax.random.key(seed)
        ks = jax.random.split(key, 6)
        C, E, H = (N_EMBD, NUM_EXPERTS, 4 * N_EMBD)
        x = jax.random.normal(ks[0], (4, 256, C), dtype=jnp.float32)
        router_w = 0.02 * jax.random.normal(ks[1], (E, C), dtype=jnp.float32)
        w1 = 0.02 * jax.random.normal(ks[2], (E, H, C), dtype=jnp.float32)
        b1 = jnp.zeros((E, H), dtype=jnp.float32)
        w2 = 0.02 * jax.random.normal(ks[3], (E, C, H), dtype=jnp.float32)
        b2 = jnp.zeros((E, C), dtype=jnp.float32)
        return {'x': x, 'router_w': router_w, 'w1': w1, 'b1': b1, 'w2': w2, 'b2': b2}
    _L0_ffn_in = _L0_ffn_setup()
    _d = {'L0_attn_x': _L0_attn_in['x'], 'L0_attn_Wq': _L0_attn_in['Wq'], 'L0_attn_bq': _L0_attn_in['bq'], 'L0_attn_Wk': _L0_attn_in['Wk'], 'L0_attn_bk': _L0_attn_in['bk'], 'L0_attn_Wv': _L0_attn_in['Wv'], 'L0_attn_bv': _L0_attn_in['bv'], 'L0_attn_gamma': _L0_attn_in['gamma'], 'L0_ffn_router_w': _L0_ffn_in['router_w'], 'L0_ffn_w1': _L0_ffn_in['w1'], 'L0_ffn_b1': _L0_ffn_in['b1'], 'L0_ffn_w2': _L0_ffn_in['w2'], 'L0_ffn_b2': _L0_ffn_in['b2']}
    _x0 = _d['L0_attn_x']
    _d['L0_attn_x'] = jax.random.normal(jax.random.fold_in(jax.random.key(seed), 1), (16, 256, 128), dtype=_x0.dtype)
    del _x0
    return _d

def reference(L0_attn_x, L0_attn_Wq, L0_attn_bq, L0_attn_Wk, L0_attn_bk, L0_attn_Wv, L0_attn_bv, L0_attn_gamma, L0_ffn_router_w, L0_ffn_w1, L0_ffn_b1, L0_ffn_w2, L0_ffn_b2):

    def _L0_attn_ref(x, Wq, bq, Wk, bk, Wv, bv, gamma):
        import jax, jax.numpy as jnp
        import numpy as np
        EPS = 1e-06

        def _l2_norm(t):
            inv = 1.0 / jnp.linalg.norm(t, ord=2, axis=-2)
            return t * inv[:, None, :]
        B, C, L = x.shape
        Q = x @ Wq.T + bq
        K = x @ Wk.T + bk
        V = x @ Wv.T + bv
        Q = jnp.transpose(_l2_norm(Q), (0, 2, 1))
        K = _l2_norm(K)
        tailor_sum = 1.0 / (L + jnp.einsum('bnc,bc->bn', Q, jnp.sum(K, axis=-1) + EPS))
        value_sum = jnp.sum(V, axis=-1)[:, :, None]
        matrix = jnp.einsum('bmn,bcn->bmc', K, V)
        matrix_sum = value_sum + jnp.einsum('bnm,bmc->bcn', Q, matrix)
        weight_value = matrix_sum * tailor_sum[:, None, :]
        return x + gamma * weight_value

    def _L0_ffn_ref(x, router_w, w1, b1, w2, b2):
        import jax, jax.numpy as jnp
        import numpy as np
        N_EMBD = 128
        NUM_EXPERTS = 8
        TOP_K = 2

        def new_gelu(x):
            c = jnp.sqrt(2.0 / jnp.pi).astype(x.dtype)
            return 0.5 * x * (1.0 + jnp.tanh(c * (x + 0.044715 * x ** 3)))
        B, T, C = x.shape
        E = router_w.shape[0]
        x_flat = x.reshape(B * T, C)
        router_logits = x_flat @ router_w.T
        router_probs = jax.nn.softmax(router_logits, axis=-1)
        top_k_probs, top_k_idx = jax.lax.top_k(router_probs, TOP_K)
        top_k_probs = top_k_probs / (top_k_probs.sum(axis=-1, keepdims=True) + 1e-08)
        cw = (jax.nn.one_hot(top_k_idx, E, dtype=x.dtype) * top_k_probs[..., None]).sum(axis=1)
        output = jnp.zeros_like(x_flat)
        for e in range(E):
            h = new_gelu(x_flat @ w1[e].T + b1[e])
            out_e = h @ w2[e].T + b2[e]
            output = output + cw[:, e:e + 1] * out_e
        return output.reshape(B, T, C)
    x = L0_attn_x
    x = _layernorm(x + _L0_attn_ref(x, L0_attn_Wq, L0_attn_bq, L0_attn_Wk, L0_attn_bk, L0_attn_Wv, L0_attn_bv, L0_attn_gamma), axis=-1)
    x = _layernorm(x + _L0_ffn_ref(x, L0_ffn_router_w, L0_ffn_w1, L0_ffn_b1, L0_ffn_w2, L0_ffn_b2), axis=-1)
    return x

_drawn_inputs = setup_inputs


def setup_inputs(seed=0):
    import zlib

    import numpy as np

    out = dict(_drawn_inputs(seed))
    spreads = {'L0_attn_bq': (0.0, 2.0),
     'L0_attn_bk': (0.0, 2.0),
     'L0_attn_bv': (0.0, 2.0),
     'L0_ffn_b1': (0.0, 0.466),
     'L0_ffn_b2': (0.0, 0.1)}
    factors = {'L0_attn_Wq': 61.321, 'L0_attn_Wk': 59.712, 'L0_attn_Wv': 63.23}
    for name, (base, spread) in spreads.items():
        noise = np.random.default_rng([zlib.crc32(name.encode()), seed]).standard_normal(out[name].shape)
        drawn = base * np.exp(spread * noise) if base else spread * noise
        out[name] = jnp.asarray(drawn.astype(out[name].dtype))
    for name, factor in factors.items():
        out[name] = (out[name] * factor).astype(out[name].dtype)
    return out
```

```python
from contextlib import ExitStack

import numpy as np

import concourse.bass as bass
from concourse import mybir

P = 128
B, C, D = 16, 256, 128
TOK = B * C
E = 8
H = 4 * D
HC = H // P
NT = TOK // P
GB = 2
T = GB * C // P
G = B // GB
GC = T * P
SLOTS = 512
SJ = SLOTS // P
TILES = (2 * TOK - E) // SLOTS + E
REG = TOK + SLOTS
ROW = D + 2
SKIP = 1 << 20
EPS_K = 1e-6
EPS_LN = 1e-5
NEG = -1e30
ACT_GELU = "gelu_apprx_tanh_and_others"
ACT_LN_EXP = "natural_log_exp_and_others"

F32 = mybir.dt.float32
F32R = mybir.dt.float32r
BF16 = mybir.dt.bfloat16
I32 = mybir.dt.int32
ALU = mybir.AluOpType
ACT = mybir.ActivationFunctionType
AX = mybir.AxisListType

K_ID, K_TRI, K_REV, K_BASE = 0, P, 2 * P, 2 * P + T * E
K_THR = K_BASE + E
K_T = K_THR + E * (TOK // SLOTS)
K_TS = K_T + TILES * E
K_COLS = K_TS + TILES
RING = 4


def moe_layer(nc, x, xT, wqkT, wvT, bqk, bv, gamma, rwT, wts, bcols, consts, returns, out,
              regions, returned):
    with ExitStack() as ctx:
        def sb(name, shape, dt=F32):
            return ctx.enter_context(nc.sbuf_tensor(name, shape, dt))

        def psum(name, shape):
            return ctx.enter_context(nc.psum_tensor(name, shape, F32))

        def sem(name):
            return ctx.enter_context(nc.semaphore(name))

        bank = psum("bank", [P, 8, 512])
        qk_ps = bank[:, 0:2, :]
        vT_ps = bank[:, 2, :]
        kq_ps = bank[:, 3, 0:GB * D].rearrange("p (b n) -> p b n", b=GB)
        qss_ps = bank[:, 4, 0:GB * D].rearrange("p (b n) -> p b n", b=GB)
        kss_ps = bank[:, 4, GB * D:GB * D + GB]
        ss_ps = bank[:, 4, 0:GB * D + GB]
        att_ps = bank[:, 5, :]
        x1T_ps = bank[:, 6, :]
        lg_ps = bank[:, 7, 0:T * E].rearrange("p (t e) -> p t e", t=T)
        rk_ps = bank[:, 7, 64:64 + T * E].rearrange("p (t e) -> p t e", t=T)
        tot_ps = bank[:, 7, 128:128 + E]

        k_sb = sb("k_sb", [P, K_COLS])
        ident = k_sb[:, K_ID:K_ID + P]
        rev = k_sb[:, K_REV:K_REV + T * E].rearrange("p (t e) -> p t e", t=T)
        ret_sb = sb("ret_sb", [P, G, 2, T], I32)
        wqk_sb = sb("wqk_sb", [P, 2 * D])
        wv_sb = sb("wv_sb", [P, D])
        bqk_sb = sb("bqk_sb", [P, 2 * D])
        bv_sb = sb("bv_sb", [P, 1])
        gam_sb = sb("gam_sb", [P, 1])
        gam2 = sb("gam2", [P, 1])
        rw_sb = sb("rw_sb", [P, E])
        bcol_sb = sb("bcol_sb", [P, E, HC + 1])
        ones = sb("ones", [P, P])
        epsm = sb("epsm", [P, P])
        tri16 = sb("tri16", [P, P], BF16)
        ones16 = sb("ones16", [P, P], BF16)

        x_sb = sb("x_sb", [P, 2, T * D])
        xT_sb = sb("xT_sb", [P, 2, GC])
        work = sb("work", [P, 2, T * 2 * D])
        qk = work[:, 0, :].rearrange("p (t n) -> p t n", t=T)
        qk2 = work[:, 1, :].rearrange("p (t n) -> p t n", t=T)
        vT = sb("vT", [P, GC])
        lnss = sb("lnss", [P, GB * D + GB])
        inv = sb("inv", [P, GB * D + GB])
        invq = inv[:, 0:GB * D].rearrange("p (b n) -> p b n", b=GB)
        invk = inv[:, GB * D:GB * D + GB]
        g1 = sb("g1", [P, GB, D])
        den = sb("den", [P, GB, D])
        tail = sb("tail", [P, GB, D])
        gq = sb("gq", [P, GB, D])
        mm = sb("mm", [P, GB, D])
        z = sb("z", [P, T, D])
        st6 = sb("st6", [P, T, 6])
        mv = sb("mv", [P, T, 2])
        mv2 = sb("mv2", [P, 2, T, 2])
        var = sb("var", [P, T])
        lnv = sb("lnv", [P, T])
        rstd0 = sb("rstd0", [P, T])
        nwt = sb("nwt", [P, T])
        nwt2 = sb("nwt2", [P, T])
        rstd = sb("rstd", [P, T])
        nmr = sb("nmr", [P, T])
        rows = sb("rows", [P, 2, 2, T, ROW])
        rows_i = rows[:, :, :, :, :].bitcast(I32)
        x1T = sb("x1T", [P, GC])
        x1_all = sb("x1_all", [P, NT, D])

        m1 = sb("m1", [P, T])
        dl = sb("dl", [P, T, E])
        key1 = sb("key1", [P, T, E])
        km1 = sb("km1", [P, T])
        oh12 = sb("oh12", [P, 2, T, E])
        dl2 = sb("dl2", [P, T, E])
        m2 = sb("m2", [P, T])
        eq2 = sb("eq2", [P, T, E])
        key2 = sb("key2", [P, T, E])
        km2 = sb("km2", [P, T])
        oh16 = sb("oh16", [P, T, E], BF16)
        base = sb("base", [P, 2, E])
        place = sb("place", [P, T, E])
        sel = sb("sel", [P, 2, T, E])
        pos = sb("pos", [P, 2, 2, T], I32)
        ex = sb("ex", [P, T, E])
        ex2 = sb("ex2", [P, T])
        zs = sb("zs", [P, T])
        rz = sb("rz", [P, T])
        p2 = sb("p2", [P, T])
        ps_ = sb("ps_", [P, T])
        rs = sb("rs", [P, T])

        NF = TOK // SLOTS
        thr = k_sb[:, K_THR:K_THR + E * NF].rearrange("p (e n) -> p e n", e=E)
        tno = k_sb[:, K_T:K_T + TILES * E].rearrange("p (t e) -> p t e", t=TILES)
        tsl = k_sb[:, K_TS:K_TS + TILES]
        cnt = sb("cnt", [P, E])
        over = sb("over", [P, E, NF])
        ntile = sb("ntile", [P, E])
        cum = sb("cum", [P, E])
        past = sb("past", [P, TILES, E])
        pastn = sb("pastn", [P, TILES, E])
        tex = sb("tex", [P, TILES])
        tst = sb("tst", [P, TILES])
        toff = sb("toff", [P, TILES])
        trow = sb("trow", [P, TILES])
        row_i = sb("row_i", [P, TILES], I32)
        exp_i = sb("exp_i", [P, TILES], I32)
        pad_i = sb("pad_i", [P, E], I32)

        h_ps = bank[:, 0:HC, :]
        xg_ps = bank[:, 4, :]
        y_ps = bank[:, 5, :]
        yt_ps = bank[:, 6, :]
        pad_sb = sb("pad_sb", [P, SJ, ROW])
        wraw = sb("wraw", [P, 2, H])
        wsp = sb("wsp", [P, E, 2, 2, H], F32R)
        w1st = sb("w1st", [P, 2, 2, H], F32R)
        w2st = sb("w2st", [P, 2, 2, H], F32R)
        bst = sb("bst", [P, RING, HC + 1])
        xg = sb("xg", [P, RING, SJ, ROW])
        xh = sb("xh", [P, SLOTS], F32R)
        xl = sb("xl", [P, SLOTS], F32R)
        h_sb = work[:, :, :].rearrange("p a (m s) -> p (a m) s", s=SLOTS)
        hh = sb("hh", [P, 2, HC, SLOTS], F32R)
        hl = sb("hl", [P, 2, HC, SLOTS], F32R)
        y_sb = sb("y_sb", [P, SLOTS])
        yo = sb("yo", [P, 2, SJ, D])
        back = sb("back", [P, RING, SJ, 2])

        s_const = sem("s_const")
        s_x = [sem("s_x0"), sem("s_x1")]
        s_xT = [sem("s_xT0"), sem("s_xT1")]
        s_set = sem("s_set")
        (s_qk, s_vT, s_kq, s_stat, s_den, s_att, s_xt, s_lg, s_rk) = [sem("pe_" + n) for n in (
            "qk", "vT", "kq", "stat", "den", "att", "xt", "lg", "rk")]
        (a_lnv, a_rstd, a_x1, a_vT, a_sq, a_lnss, a_inv, a_x1T, a_g1, a_rowb, a_ex) = [sem("act_" + n) for n in (
            "lnv", "rstd", "x1", "vT", "sq", "lnss", "inv", "x1T", "g1", "rowb", "ex")]
        (v_z, v_st, v_mv, v_var, v_nwt, v_nwt2, v_rstd, v_nmr, v_qk, v_den, v_den2, v_gq, v_tail, v_mm, v_m1,
         v_dl, v_key1, v_km1, v_oh1, v_dl2, v_m2, v_eq2, v_key2, v_km2, v_oh2, v_oh, v_place,
         v_base, v_sel, v_pos, v_zs, v_rz, v_p2, v_ps, v_rs, v_row) = [sem("dve_" + n) for n in (
            "z", "st", "mv", "var", "nwt", "nwt2", "rstd", "nmr", "qk", "den", "den2", "gq", "tail", "mm", "m1",
            "dl", "key1", "km1", "oh1", "dl2", "m2", "eq2", "key2", "km2", "oh2", "oh", "place",
            "base", "sel", "pos", "zs", "rz", "p2", "ps", "rs", "row")]
        s_scat = [sem("s_scat0"), sem("s_scat1")]
        s_keep = [sem("s_keep0"), sem("s_keep1")]
        s_done = [sem("s_done0"), sem("s_done1")]
        s_pad0 = sem("s_pad0")
        s_wraw = [sem("s_wraw0"), sem("s_wraw1")]
        s_whi, s_wlo = sem("s_whi"), sem("s_wlo")
        v_tab = sem("dve_table")
        g_turn = sem("pool_turn")
        v_chain = sem("dve_chain")
        s_pads = sem("s_pads")
        s_tile = [sem(f"s_tile{r}") for r in range(RING)]
        s_bst = [sem(f"s_bst{r}") for r in range(RING)]
        s_w1 = [sem("s_w1st0"), sem("s_w1st1")]
        s_w2 = [sem("s_w2st0"), sem("s_w2st1")]
        p_xg, p_h, p_y, p_yt = [sem("pe_" + n) for n in ("xg", "h", "y", "ytr")]
        a_h, a_y, a_yo = [sem("act_" + n) for n in ("h", "y", "yo")]
        v_pad, v_xh, v_xl, v_hh, v_hl, v_back = [sem("dve_" + n) for n in ("pad", "xh", "xl", "hh", "hl", "back")]
        s_ret = [sem(f"s_ret{r}") for r in range(RING)]
        s_y1 = [sem("s_y10"), sem("s_y11")]
        s_y2 = [sem("s_y20"), sem("s_y21")]
        (f_z1, f_z, f_st, f_mv, f_var, f_nwt, f_nwt2, f_rstd, f_nmr) = [sem("fin_" + n) for n in (
            "z1", "z", "st", "mv", "var", "nwt", "nwt2", "rstd", "nmr")]
        g_lnv, g_rstd, g_out = [sem("fina_" + n) for n in ("lnv", "rstd", "out")]
        CONST = 16 * 9

        block = ctx.enter_context(nc.Block())

        def steps(eng, step):
            step(0, None, 0)
            step(1, 0, 1)
            step(2, 1, 0)
            with eng.Fori(1, G // 2 - 1) as i:
                step(2 * i + 1, 2 * i, 1)
                step(2 * i + 2, 2 * i + 1, 0)
            step(G - 1, G - 2, 1)
            step(None, G - 1, 0)

        def after(eng, s, n):
            if not isinstance(n, int) or n > 0:
                eng.wait_ge(s, n)

        def tiles(eng, step):
            last = (TILES - 3) // RING
            for t in range(RING + 1):
                step(t, t // RING, t % RING)
            with eng.Fori(1, last) as i:
                for k in range(1, RING + 1):
                    step(RING * i + k, i + k // RING, k % RING)
            for t in range(RING * last + 1, TILES + 2):
                step(t, t // RING, t % RING)

        def within(t):
            return not isinstance(t, int) or 0 <= t < TILES

        def free(eng, b, par):
            n = b // 2 if isinstance(b, int) else None
            if n is None:
                if par == 0:
                    eng.wait_ge(s_scat[par], 64 * b)
                    eng.wait_ge(s_keep[par], 8 * b)
                else:
                    eng.wait_ge(s_scat[par], 64 * b - 64)
                    eng.wait_ge(s_keep[par], 8 * b - 8)
            elif n > 0:
                eng.wait_ge(s_scat[par], 128 * n)
                eng.wait_ge(s_keep[par], 16 * n)

        @block.sync
        def _(sp):
            loads = [(k_sb[:, :], consts), (wqk_sb[:, :], wqkT), (wv_sb[:, :], wvT),
                     (bqk_sb[:, :], bqk.partition_broadcast(P)), (bv_sb[:, :], bv),
                     (gam_sb[:, :], gamma.partition_broadcast(P)), (rw_sb[:, :], rwT),
                     (bcol_sb[:, :, :], bcols), (ret_sb[:, :, :, :], returns)]
            x_groups = x.rearrange("(g t p) d -> g p t d", t=T, p=P)
            xT_groups = xT.rearrange("d (g n) -> g d n", n=GC)

            def load(g, par, n):
                after(sp, s_vT, g - 1)
                sp.dma_start(xT_sb[:, par, :], xT_groups[g]).then_inc(s_xT[par], 16)
                after(sp, v_z, g - 1)
                sp.dma_start(x_sb[:, par, :].rearrange("p (t d) -> p t d", t=T), x_groups[g]).then_inc(s_x[par], 16)

            load(0, 0, 0)
            for dst, src in loads:
                sp.dma_start(dst, src).then_inc(s_const, 16)
            load(1, 1, 0)
            sp.wait_ge(v_pad, 2)
            sp.dma_start(regions[E * REG:E * REG + SLOTS, :].rearrange("(p j) c -> p j c", j=SJ),
                         pad_sb[:, :, :]).then_inc(s_pad0, 16)
            with sp.Fori(1, G // 2) as i:
                sp.wait_ge(s_vT, 2 * i - 1)
                sp.dma_start(xT_sb[:, 0, :], xT_groups[bass.ds(2 * i, 1)].rearrange("o d n -> d (o n)")).then_inc(s_xT[0], 16)
                sp.wait_ge(v_z, 2 * i - 1)
                sp.dma_start(x_sb[:, 0, :].rearrange("p (t d) -> p t d", t=T),
                             x_groups[bass.ds(2 * i, 1)].rearrange("o p t d -> p (o t) d")).then_inc(s_x[0], 16)
                sp.wait_ge(s_vT, 2 * i)
                sp.dma_start(xT_sb[:, 1, :], xT_groups[bass.ds(2 * i + 1, 1)].rearrange("o d n -> d (o n)")).then_inc(s_xT[1], 16)
                sp.wait_ge(v_z, 2 * i)
                sp.dma_start(x_sb[:, 1, :].rearrange("p (t d) -> p t d", t=T),
                             x_groups[bass.ds(2 * i + 1, 1)].rearrange("o p t d -> p (o t) d")).then_inc(s_x[1], 16)
            for n in range(2 * E):
                after(sp, s_wlo, n - 1)
                sp.dma_start(wraw[:, n % 2, :], wts[:, n // 2, n % 2, :]).then_inc(s_wraw[n % 2], 16)
            sp.wait_ge(v_tab, 3)
            for e in range(E):
                row = sp.value_load(pad_i[0:1, e:e + 1], min_val=e * REG, max_val=e * REG + TOK)
                sp.dma_start(regions[bass.ds(row, SLOTS), :].rearrange("(p j) c -> p j c", j=SJ),
                             pad_sb[:, :, :]).then_inc(s_pads, 16)
            for q in range(2):
                sp.wait_ge(s_scat[q], 128 * (G // 2))
                sp.wait_ge(s_keep[q], 16 * (G // 2))
            sp.wait_ge(s_pads, 16 * E)
            sp.wait_ge(s_pad0, 16)
            sp.wait_ge(s_wlo, 2 * E)

            def load_tile(t, n, r):
                after(sp, v_back, t - RING + 1)
                row = sp.value_load(row_i[0:1, t:t + 1] if isinstance(t, int) else row_i[0:1, bass.ds(t, 1)],
                                    min_val=0, max_val=E * REG)
                sp.dma_start(xg[:, r, :, :], regions[bass.ds(row, SLOTS), :].rearrange("(p j) c -> p j c", j=SJ)
                             ).then_inc(s_tile[r], 16)

            def load_step(t, n, r):
                if isinstance(t, int) and t == 0:
                    load_tile(0, 0, 0)
                    load_tile(1, 0, 1)
                if within(t) and (not isinstance(t, int) or t + 2 < TILES):
                    load_tile(t + 2, None, (r + 2) % RING)
                if within(t):
                    e = sp.value_load(exp_i[0:1, t:t + 1] if isinstance(t, int) else exp_i[0:1, bass.ds(t, 1)],
                                      min_val=0, max_val=E - 1)
                    after(sp, p_h, HC * (t - 1))
                    sp.dma_start(w1st[:, r % 2, :, :].bitcast(F32), wsp[:, bass.ds(e, 1), 0, :, :].bitcast(F32).rearrange("p o a h -> p (o a) h")
                                 ).then_inc(s_w1[r % 2], 16)
                    after(sp, a_y, t - RING + 1)
                    sp.dma_start(bst[:, r, :], bcol_sb[:, bass.ds(e, 1), :].rearrange("p o a -> p (o a)")
                                 ).then_inc(s_bst[r], 16)
                    after(sp, p_y, t - 1)
                    sp.dma_start(w2st[:, r % 2, :, :].bitcast(F32), wsp[:, bass.ds(e, 1), 1, :, :].bitcast(F32).rearrange("p o a h -> p (o a) h")
                                 ).then_inc(s_w2[r % 2], 16)

            tiles(sp, load_step)

            for r in range(RING):
                sp.wait_ge(s_ret[r], 16 * SJ * len(range(r, TILES, RING)))
            ret = returned.rearrange("(k g t p) d -> k g p t d", k=2, t=T, p=P)
            outg = out.rearrange("(g t p) d -> g p t d", t=T, p=P)
            for c in range(G + 2):
                q = c % 2
                if c < G:
                    after(sp, f_z, c - 1)
                    sp.dma_start(x_sb[:, q, :].rearrange("p (t d) -> p t d", t=T), ret[0, c]).then_inc(s_y1[q], 16)
                    sp.dma_start(xT_sb[:, q, :].rearrange("p (t d) -> p t d", t=T), ret[1, c]).then_inc(s_y2[q], 16)
                if c >= 2:
                    sp.wait_ge(g_out, c - 1)
                    sp.dma_start(outg[c - 2], x1_all[:, T * (c - 2):T * (c - 1), :]).then_inc(s_done[q], 16)
            for q in range(2):
                sp.wait_ge(s_done[q], 16 * (G // 2))

        @block.tensor
        def _(pe):
            def step(f, b, par):
                if b is not None:
                    pe.wait_ge(v_mm, b + 1)
                    after(pe, v_z, b)
                    for t in range(T):
                        last = nc.tensor.matmul(att_ps[:, t * D:(t + 1) * D], vT[:, t * P:(t + 1) * P],
                                                mm[:, t * P // C, :], start=True, stop=True)
                    last.then_inc(s_att, 1)
                if f is not None:
                    if isinstance(f, int) and f == 0:
                        pe.wait_ge(s_const, CONST)
                        pe.wait_ge(s_set, 4)
                    loads = (f // 2 + 1) if isinstance(f, int) else None
                    pe.wait_ge(s_xT[par], 16 * loads if loads else 8 * (f + 2 - par))
                    after(pe, v_qk, f)
                    for t in range(T):
                        last = nc.tensor.matmul(qk_ps[:, t * P // C, t % 2 * 2 * D:(t % 2 + 1) * 2 * D],
                                                xT_sb[:, par, t * P:(t + 1) * P], wqk_sb[:, :],
                                                start=True, stop=True)
                    last.then_inc(s_qk, 1)
                    after(pe, a_vT, f)
                    nc.tensor.matmul(vT_ps, wv_sb[:, :], xT_sb[:, par, :], start=True, stop=True).then_inc(s_vT, 1)
                if f is not None:
                    pe.wait_ge(v_qk, f + 1)
                    after(pe, v_den, f)
                    for t in range(T):
                        last = nc.tensor.matmul(kq_ps[:, t * P // C, :], qk[:, t, D:2 * D], qk[:, t, 0:D],
                                                start=t * P % C == 0, stop=(t + 1) * P % C == 0)
                    last.then_inc(s_kq, 1)
                    pe.wait_ge(a_sq, f + 1)
                    after(pe, a_lnss, f)
                    for t in range(T):
                        nc.tensor.matmul(qss_ps[:, t * P // C, :], ones[:, :], qk2[:, t, 0:D],
                                         start=t * P % C == 0, stop=(t + 1) * P % C == 0)
                    for t in range(T):
                        b0 = t * P // C
                        last = nc.tensor.matmul(kss_ps[:, b0:b0 + 1], qk2[:, t, D:2 * D], ones[:, 0:1],
                                                start=t * P % C == 0, stop=(t + 1) * P % C == 0)
                    last.then_inc(s_stat, 1)
                if b is not None:
                    pe.wait_ge(a_x1, b + 1)
                    after(pe, a_x1T, b)
                    for t in range(T):
                        last = nc.tensor.transpose(x1T_ps[:, t * P:(t + 1) * P], rows[:, 1 - par, 0, t, 0:D], ident)
                    last.then_inc(s_xt, 1)
                if b is not None:
                    pe.wait_ge(a_x1T, b + 1)
                    after(pe, v_base, b)
                    for t in range(T):
                        last = nc.tensor.matmul(lg_ps[:, t, :], x1T[:, t * P:(t + 1) * P], rw_sb[:, :],
                                                start=True, stop=True)
                    last.then_inc(s_lg, 1)
                if f is not None:
                    pe.wait_ge(a_g1, f + 1)
                    for q in range(GB):
                        for t in range(q * C // P, (q + 1) * C // P):
                            nc.tensor.matmul(kq_ps[:, q, :], epsm[:, :], qk[:, t, 0:D],
                                             start=t * P % C == 0, stop=False)
                        last = nc.tensor.matmul(kq_ps[:, q, :], ones[:, :], g1[:, q, :], start=False, stop=True)
                    last.then_inc(s_den, 1)
                if b is not None:
                    pe.wait_ge(v_oh, b + 1)
                    nc.tensor.matmul(rk_ps[:, :, :], tri16[:, :], oh16[:, :, :], start=True, stop=True)
                    for t in range(T - 1):
                        for u in range(t + 1, T):
                            nc.tensor.matmul(rk_ps[:, u, :], ones16[:, :], oh16[:, t, :], start=False,
                                             stop=True, skip_group_check=True)
                    for t in range(T):
                        last = nc.tensor.matmul(tot_ps, ones16[:, :], oh16[:, t, :], start=t == 0, stop=t == T - 1,
                                                skip_group_check=True)
                    last.then_inc(s_rk, 1)

            steps(pe, step)

            def tile_step(t, n, r):
                par = r % 2
                int_t = isinstance(t, int)

                def transposed(t, n, r):
                    pe.wait_ge(s_tile[r], 16 * (n + 1))
                    after(pe, v_xl, t)
                    for j in range(SJ):
                        last = nc.tensor.transpose(xg_ps[:, j * P:(j + 1) * P], xg[:, r, j, 0:D], ident)
                    last.then_inc(p_xg, 1)

                if int_t and t == 0:
                    pe.wait_ge(v_base, G)
                    pe.wait_ge(a_x1T, G)
                    pe.wait_ge(v_z, G)
                    pe.wait_ge(v_mm, G)
                    transposed(0, 0, 0)
                if within(t):
                    pe.wait_ge(s_w1[par], 16 * (t // 2 + 1) if int_t else 8 * (t - par) + 16)
                    pe.wait_ge(v_xl, t + 1)
                    for m in range(HC):
                        cols = slice(m * P, (m + 1) * P)
                        after(pe, a_h, HC * (t - 1) + m + 1)
                        nc.tensor.matmul(h_ps[:, m, :], w1st[:, par, 0, cols], xh[:, :], start=True, stop=False)
                        nc.tensor.matmul(h_ps[:, m, :], w1st[:, par, 0, cols], xl[:, :], start=False, stop=False)
                        nc.tensor.matmul(h_ps[:, m, :], w1st[:, par, 1, cols], xh[:, :], start=False, stop=True
                                         ).then_inc(p_h, 1)
                if within(t) and (not int_t or t + 1 < TILES):
                    transposed(t + 1, n + (r == RING - 1), (r + 1) % RING)
                if (not int_t or t >= 2) and (not int_t or t - 2 < TILES):
                    pe.wait_ge(a_y, t - 1)
                    after(pe, a_yo, t - 2)
                    for j in range(SJ):
                        last = nc.tensor.transpose(yt_ps[:, j * P:(j + 1) * P], y_sb[:, j * P:(j + 1) * P], ident)
                    last.then_inc(p_yt, 1)
                if (not int_t or 1 <= t <= TILES):
                    pe.wait_ge(s_w2[1 - par], 16 * ((t - 1) // 2 + 1) if int_t else 8 * (t + par))
                    after(pe, a_y, t - 1)
                    for m in range(HC):
                        cols = slice(m * P, (m + 1) * P)
                        pe.wait_ge(v_hl, HC * (t - 1) + m + 1)
                        nc.tensor.matmul(y_ps, w2st[:, 1 - par, 0, cols], hh[:, 1 - par, m, :], start=m == 0, stop=False)
                        nc.tensor.matmul(y_ps, w2st[:, 1 - par, 0, cols], hl[:, 1 - par, m, :], start=False, stop=False)
                        last = nc.tensor.matmul(y_ps, w2st[:, 1 - par, 1, cols], hh[:, 1 - par, m, :], start=False,
                                                stop=m == HC - 1)
                    last.then_inc(p_y, 1)

            tiles(pe, tile_step)

        @block.scalar
        def _(act):
            def step(f, b, par):
                if b is not None:
                    act.wait_ge(v_var, b + 1)
                    nc.scalar.activation(lnv[:, :], var[:, :], ACT.Ln).then_inc(a_lnv, 1)
                    act.wait_ge(a_lnv, b + 1)
                    after(act, v_rstd, b)
                    nc.scalar.activation(rstd0[:, :], lnv[:, :], ACT.Exp, scale=-0.5).then_inc(a_rstd, 1)
                if f is not None:
                    if isinstance(f, int) and f == 0:
                        act.wait_ge(s_const, CONST)
                    act.wait_ge(s_vT, f + 1)
                    after(act, s_att, f)
                    nc.scalar.activation(vT[:, :], vT_ps, ACT.Identity, bias=bv_sb[:, 0:1]).then_inc(a_vT, 1)
                    act.wait_ge(v_qk, f + 1)
                    after(act, s_stat, f)
                    nc.scalar.activation(qk2, qk, ACT.Square).then_inc(a_sq, 1)
                if b is not None:
                    act.wait_ge(v_nmr, b + 1)
                    free(act, b, 1 - par)
                    for t in range(T):
                        last = nc.scalar.activation(rows[:, 1 - par, 0, t, 0:D], z[:, t, :], ACT.Identity,
                                                    bias=nmr[:, t:t + 1], scale=rstd[:, t:t + 1])
                    last.then_inc(a_x1, 1)
                if f is not None:
                    act.wait_ge(s_stat, f + 1)
                    nc.scalar.activation(lnss[:, :], ss_ps, ACT.Ln).then_inc(a_lnss, 1)
                    act.wait_ge(a_lnss, f + 1)
                    after(act, v_mm, f)
                    nc.scalar.activation(inv[:, :], lnss[:, :], ACT.Exp, scale=-0.5).then_inc(a_inv, 1)
                if b is not None:
                    act.wait_ge(s_xt, b + 1)
                    after(act, s_lg, b)
                    nc.scalar.copy(x1T[:, :], x1T_ps).then_inc(a_x1T, 1)
                if f is not None:
                    act.wait_ge(s_kq, f + 1)
                    act.wait_ge(a_inv, f + 1)
                    after(act, v_gq, f)
                    after(act, s_den, f)
                    for q in range(GB):
                        last = nc.scalar.activation(g1[:, q, :], kq_ps[:, q, :], ACT.Copy, scale=invk[:, q:q + 1])
                    last.then_inc(a_g1, 1)
                if b is not None:
                    act.wait_ge(a_x1, b + 1)
                    nc.scalar.copy(rows[:, 1 - par, 1, :, 0:D], rows[:, 1 - par, 0, :, 0:D]).then_inc(a_rowb, 1)
                    act.wait_ge(v_m2, b + 1)
                    after(act, v_p2, b)
                    nc.scalar.activation(ex[:, :, :], dl[:, :, :], ACT.Exp)
                    nc.scalar.activation(ex2[:, :], m2[:, :], ACT.Exp).then_inc(a_ex, 1)

            act.preload_act_table_set(ACT_LN_EXP)
            steps(act, step)
            act.preload_act_table_set(ACT_GELU)

            def tile_step(t, n, r):
                int_t = isinstance(t, int)
                if (not int_t or 1 <= t - 1 <= TILES):
                    act.wait_ge(p_y, t - 1)
                    after(act, p_yt, t - 2)
                    nc.scalar.activation(y_sb[:, :], y_ps, ACT.Identity, bias=bst[:, (r - 2) % RING, HC:HC + 1]
                                         ).then_inc(a_y, 1)
                if within(t):
                    act.wait_ge(s_bst[r], 16 * (n + 1))
                    for m in range(HC):
                        act.wait_ge(p_h, HC * t + m + 1)
                        after(act, v_hl, HC * (t - 1) + m + 1)
                        nc.scalar.activation(h_sb[:, m, :], h_ps[:, m, :], ACT.Gelu_apprx_tanh, bias=bst[:, r, m:m + 1]
                                             ).then_inc(a_h, 1)
                if (not int_t or 0 <= t - 2 < TILES):
                    act.wait_ge(p_yt, t - 1)
                    act.wait_ge(v_back, t - 1)
                    if not int_t:
                        act.wait_ge(s_ret[r % 4], 16 * SJ * n)
                    elif t >= 4:
                        act.wait_ge(s_ret[r % 4], 16 * SJ * (t // 4))
                    for j in range(SJ):
                        last = nc.scalar.activation(yo[:, r % 2, j, :], yt_ps[:, j * P:(j + 1) * P], ACT.Copy,
                                                    scale=back[:, (r - 2) % RING, j, 1:2])
                    last.then_inc(a_yo, 1)

            tiles(act, tile_step)
            act.preload_act_table_set(ACT_LN_EXP)
            for c in range(G + 1):
                if c < G:
                    act.wait_ge(f_var, c + 1)
                    nc.scalar.activation(lnv[:, :], var[:, :], ACT.Ln).then_inc(g_lnv, 1)
                    act.wait_ge(g_lnv, c + 1)
                    after(act, f_rstd, c)
                    nc.scalar.activation(rstd0[:, :], lnv[:, :], ACT.Exp, scale=-0.5).then_inc(g_rstd, 1)
                if c >= 1:
                    act.wait_ge(f_nmr, c)
                    for t in range(T):
                        u = T * (c - 1) + t
                        last = nc.scalar.activation(x1_all[:, u, :], x1_all[:, u, :], ACT.Identity,
                                                    bias=nmr[:, t:t + 1], scale=rstd[:, t:t + 1])
                    last.then_inc(g_out, 1)

        @block.vector
        def _(ve):
            nc.vector.memset(ones[:, :], 1.0).then_inc(s_set, 1)
            nc.vector.memset(epsm[:, :], EPS_K).then_inc(s_set, 1)
            nc.vector.memset(ones16[:, :], 1.0).then_inc(s_set, 1)
            ve.wait_ge(s_const, CONST)
            nc.vector.tensor_copy(tri16[:, :], k_sb[:, K_TRI:K_TRI + P]).then_inc(s_set, 1)
            nc.vector.tensor_scalar(gam2[:, :], gam_sb[:, :], 0.5, None, ALU.mult).then_inc(s_set, 1)
            nc.vector.tensor_copy(base[:, 0, :], k_sb[:, K_BASE:K_BASE + E]).then_inc(s_set, 1)
            ve.wait_ge(s_set, 6)
            nc.vector.memset(pad_sb[:, :, :], 0.0).then_inc(v_pad, 1)
            ve.wait_ge(v_pad, 1)
            nc.vector.memset(pad_sb[:, :, D:D + 1].bitcast(I32), SKIP).then_inc(v_pad, 1)

            def step(f, b, par):
                q = 1 - par
                if b is not None:
                    def link(ins, s):
                        ins.then_inc(s, 1)
                        ve.wait_ge(s, b + 1)
                    ve.wait_ge(s_att, b + 1)
                    ve.wait_ge(s_x[q], 16 * (b // 2 + 1) if isinstance(b, int) else 8 * (b + 2 - q))
                    after(ve, a_x1, b)
                    link(nc.vector.scalar_tensor_tensor(z[:, :, :].rearrange("p t d -> p (t d)"), att_ps,
                                                        gam2[:, 0:1], x_sb[:, q, :], ALU.mult, ALU.add), v_z)
                    for t in range(T):
                        last = nc.vector.bn_stats(st6[:, t, :], z[:, t, :])
                    link(last, v_st)
                    free(ve, b, q)
                    g = b if isinstance(b, int) else None
                    src = ret_sb[:, g] if g is not None else ret_sb[:, bass.ds(b, 1)].rearrange("p o k t -> p (o k) t")
                    nc.vector.tensor_copy(rows_i[:, q, :, :, D], src)
                    for t in range(T):
                        last = nc.vector.bn_aggr(mv[:, t, :], st6[:, t, :])
                    link(last, v_mv)
                    nc.vector.tensor_scalar(var[:, :], mv[:, :, 1], EPS_LN / 4, None, ALU.add).then_inc(v_var, 1)
                if f is not None:
                    ve.wait_ge(s_qk, f + 1)
                    after(ve, s_den, f)
                    after(ve, a_sq, f)
                    for s in range(GB):
                        last = nc.vector.tensor_tensor(
                            qk[:, 2 * s:2 * s + 2, :], qk_ps[:, s, :].rearrange("p (t n) -> p t n", t=2),
                            bqk_sb[:, :].unsqueeze(1).to_broadcast([P, 2, 2 * D]), ALU.add)
                    last.then_inc(v_qk, 1)
                if b is not None:
                    ve.wait_ge(a_rstd, b + 1)
                    ve.wait_ge(v_var, b + 1)
                    link(nc.vector.scalar_tensor_tensor(nwt[:, :], var[:, :], -0.5, rstd0[:, :], ALU.mult, ALU.mult), v_nwt)
                    link(nc.vector.tensor_tensor(nwt2[:, :], nwt[:, :], rstd0[:, :], ALU.mult), v_nwt2)
                    link(nc.vector.scalar_tensor_tensor(rstd[:, :], nwt2[:, :], 1.5, rstd0[:, :], ALU.add, ALU.mult), v_rstd)
                    nc.vector.scalar_tensor_tensor(nmr[:, :], mv[:, :, 0], -1.0, rstd[:, :],
                                                   ALU.mult, ALU.mult).then_inc(v_nmr, 1)
                    def wide(a):
                        return a.unsqueeze(2).to_broadcast([P, T, E])
                    ve.wait_ge(s_lg, b + 1)
                    link(nc.vector.tensor_reduce(m1[:, :], lg_ps[:, :, :], AX.X, ALU.max), v_m1)
                    after(ve, a_ex, b)
                    link(nc.vector.tensor_tensor(dl[:, :, :], lg_ps[:, :, :], wide(m1[:, :]), ALU.subtract), v_dl)
                    link(nc.vector.scalar_tensor_tensor(key1[:, :, :], dl[:, :, :], 0.0, rev, ALU.is_equal, ALU.mult), v_key1)
                    link(nc.vector.tensor_reduce(km1[:, :], key1[:, :, :], AX.X, ALU.max), v_km1)
                    link(nc.vector.tensor_tensor(oh12[:, 0, :, :], rev, wide(km1[:, :]), ALU.is_equal), v_oh1)
                    link(nc.vector.scalar_tensor_tensor(dl2[:, :, :], oh12[:, 0, :, :], NEG, dl[:, :, :], ALU.mult, ALU.add), v_dl2)
                    link(nc.vector.tensor_reduce(m2[:, :], dl2[:, :, :], AX.X, ALU.max), v_m2)
                    link(nc.vector.tensor_tensor(eq2[:, :, :], dl2[:, :, :], wide(m2[:, :]), ALU.is_equal), v_eq2)
                    link(nc.vector.tensor_tensor(key2[:, :, :], eq2[:, :, :], rev, ALU.mult), v_key2)
                    link(nc.vector.tensor_reduce(km2[:, :], key2[:, :, :], AX.X, ALU.max), v_km2)
                    link(nc.vector.tensor_tensor(oh12[:, 1, :, :], rev, wide(km2[:, :]), ALU.is_equal), v_oh2)
                    after(ve, s_rk, b)
                    nc.vector.tensor_tensor(oh16[:, :, :], oh12[:, 0, :, :], oh12[:, 1, :, :], ALU.add).then_inc(v_oh, 1)
                if f is not None:
                    ve.wait_ge(s_den, f + 1)
                    ve.wait_ge(a_inv, f + 1)
                    nc.vector.tensor_tensor(den[:, :, :], kq_ps[:, :, :], invq, ALU.mult).then_inc(v_den, 1)
                    nc.vector.tensor_tensor(gq[:, :, :], g1[:, :, :], invq, ALU.mult).then_inc(v_gq, 1)
                    ve.wait_ge(v_den, f + 1)
                    nc.vector.tensor_scalar(den[:, :, :], den[:, :, :], float(D), None, ALU.add).then_inc(v_den2, 1)
                    ve.wait_ge(v_den2, f + 1)
                    nc.vector.reciprocal(tail[:, :, :], den[:, :, :]).then_inc(v_tail, 1)
                    ve.wait_ge(v_gq, f + 1)
                    ve.wait_ge(v_tail, f + 1)
                    after(ve, s_att, f)
                    nc.vector.scalar_tensor_tensor(mm[:, :, :], gq[:, :, :], 1.0, tail[:, :, :],
                                                   ALU.add, ALU.mult).then_inc(v_mm, 1)
                if b is not None:
                    ve.wait_ge(s_rk, b + 1)
                    link(nc.vector.tensor_tensor(place[:, :, :], rk_ps[:, :, :],
                                                 base[:, q, :].unsqueeze(1).to_broadcast([P, T, E]), ALU.add), v_place)
                    nc.vector.tensor_tensor(base[:, 1 - q, :], base[:, q, :], tot_ps, ALU.add).then_inc(v_base, 1)
                    for k in range(2):
                        last = nc.vector.tensor_tensor(sel[:, k, :, :], oh12[:, k, :, :], place[:, :, :], ALU.mult)
                    link(last, v_sel)
                    with nc.allow_low_precision(reason="one whole number below 2^24, the rest zeros"):
                        nc.vector.tensor_reduce(pos[:, q, :, :], sel[:, :, :, :], AX.X, ALU.add).then_inc(v_pos, 1)
                    ve.wait_ge(a_ex, b + 1)
                    link(nc.vector.tensor_reduce(zs[:, :], ex[:, :, :], AX.X, ALU.add), v_zs)
                    link(nc.vector.reciprocal(rz[:, :], zs[:, :]), v_rz)
                    link(nc.vector.tensor_tensor(p2[:, :], ex2[:, :], rz[:, :], ALU.mult), v_p2)
                    link(nc.vector.scalar_tensor_tensor(ps_[:, :], p2[:, :], 1e-8, rz[:, :], ALU.add, ALU.add), v_ps)
                    link(nc.vector.reciprocal(rs[:, :], ps_[:, :]), v_rs)
                    nc.vector.tensor_tensor(rows[:, q, 0, :, D + 1], rz[:, :], rs[:, :], ALU.mult)
                    nc.vector.tensor_tensor(rows[:, q, 1, :, D + 1], p2[:, :], rs[:, :], ALU.mult).then_inc(v_row, 1)

            steps(ve, step)

            def chain(ins, n=[0]):
                ins.then_inc(v_chain, 1)
                n[0] += 1
                ve.wait_ge(v_chain, n[0])

            for e in range(E):
                for w in range(2):
                    n = 2 * e + w
                    ve.wait_ge(s_wraw[w], 16 * (e + 1))
                    ve.wait_ge(s_whi, 16)
                    nc.vector.tensor_tensor(wsp[:, e, w, 1, :], wraw[:, w, :], wsp[:, e, w, 0, :].bitcast(F32),
                                            ALU.subtract).then_inc(s_wlo, 1)

            ve.wait_ge(v_base, G)
            nc.vector.tensor_copy(pad_i[:, :], base[:, G % 2, :]).then_inc(v_tab, 1)
            chain(nc.vector.tensor_tensor(cnt[:, :], base[:, G % 2, :], k_sb[:, K_BASE:K_BASE + E], ALU.subtract))
            chain(nc.vector.tensor_tensor(over[:, :, :], cnt[:, :].unsqueeze(2).to_broadcast([P, E, NF]), thr, ALU.is_gt))
            chain(nc.vector.tensor_reduce(ntile[:, :], over[:, :, :], AX.X, ALU.add))
            chain(nc.vector.tensor_tensor_scan(cum[:, :], ones[:, 0:E], ntile[:, :], 0.0, ALU.mult, ALU.add))
            chain(nc.vector.tensor_tensor(past[:, :, :], cum[:, :].unsqueeze(1).to_broadcast([P, TILES, E]), tno, ALU.is_le))
            chain(nc.vector.tensor_tensor(pastn[:, :, :], past[:, :, :],
                                          ntile[:, :].unsqueeze(1).to_broadcast([P, TILES, E]), ALU.mult))
            chain(nc.vector.tensor_reduce(tex[:, :], past[:, :, :], AX.X, ALU.add))
            chain(nc.vector.tensor_reduce(tst[:, :], pastn[:, :, :], AX.X, ALU.add))
            chain(nc.vector.scalar_tensor_tensor(toff[:, :], tst[:, :], -float(SLOTS), tsl, ALU.mult, ALU.add))
            chain(nc.vector.scalar_tensor_tensor(trow[:, :], tex[:, :], float(REG), toff[:, :], ALU.mult, ALU.add))
            nc.vector.tensor_scalar(row_i[:, :], trow[:, :], float(E * REG), None, ALU.min).then_inc(v_tab, 1)
            nc.vector.tensor_scalar(exp_i[:, :], tex[:, :], float(E - 1), None, ALU.min).then_inc(v_tab, 1)

            def tile_step(t, n, r):
                par = r % 2
                int_t = isinstance(t, int)

                def halves(t):
                    ve.wait_ge(p_xg, t + 1)
                    after(ve, p_h, HC * t)
                    nc.vector.tensor_copy(xh[:, :], xg_ps).then_inc(v_xh, 1)
                    ve.wait_ge(v_xh, t + 1)
                    nc.vector.tensor_tensor(xl[:, :], xg_ps, xh[:, :].bitcast(F32), ALU.subtract).then_inc(v_xl, 1)

                if int_t and t == 0:
                    halves(0)
                if (not int_t or 1 <= t <= TILES):
                    ve.wait_ge(s_tile[(r - 1) % RING], 16 * ((t - 1) // RING + 1 if int_t else (n + (r > 0))))
                    if not int_t:
                        ve.wait_ge(s_ret[(r - 1) % RING], 16 * SJ * (n if r > 0 else n - 1))
                    elif t > RING:
                        ve.wait_ge(s_ret[(r - 1) % RING], 16 * SJ * ((t - 1) // RING))
                    nc.vector.tensor_copy(back[:, (r - 1) % RING, :, :].bitcast(I32), xg[:, (r - 1) % RING, :, D:D + 2].bitcast(I32)
                                          ).then_inc(v_back, 1)
                if within(t):
                    for m in range(HC):
                        ve.wait_ge(a_h, HC * t + m + 1)
                        after(ve, p_y, t - 1)
                        nc.vector.tensor_copy(hh[:, par, m, :], h_sb[:, m, :]).then_inc(v_hh, 1)
                        ve.wait_ge(v_hh, HC * t + m + 1)
                        nc.vector.tensor_tensor(hl[:, par, m, :], h_sb[:, m, :], hh[:, par, m, :].bitcast(F32),
                                                ALU.subtract).then_inc(v_hl, 1)
                        if m == 1 and (not int_t or t + 1 < TILES):
                            halves(t + 1)

            tiles(ve, tile_step)

            for c in range(G + 1):
                if c < G:
                    q = c % 2

                    def link(ins, s):
                        ins.then_inc(s, 1)
                        ve.wait_ge(s, c + 1)
                    xs = x1_all[:, T * c:T * (c + 1), :].rearrange("p t d -> p (t d)")
                    ve.wait_ge(s_y1[q], 16 * (c // 2 + 1))
                    ve.wait_ge(s_y2[q], 16 * (c // 2 + 1))
                    link(nc.vector.tensor_tensor(x_sb[:, q, :], x_sb[:, q, :], xT_sb[:, q, :], ALU.add), f_z1)
                    link(nc.vector.tensor_tensor(xs, xs, x_sb[:, q, :], ALU.add), f_z)
                    for t in range(T):
                        last = nc.vector.bn_stats(st6[:, t, :], x1_all[:, T * c + t, :])
                    link(last, f_st)
                    after(ve, f_nmr, c - 1)
                    for t in range(T):
                        last = nc.vector.bn_aggr(mv2[:, q, t, :], st6[:, t, :])
                    link(last, f_mv)
                if c >= 1:
                    ve.wait_ge(g_rstd, c)
                    after(ve, g_out, c - 1)
                    for ins, s_ in ((lambda: nc.vector.scalar_tensor_tensor(nwt[:, :], var[:, :], -0.5, rstd0[:, :], ALU.mult, ALU.mult), f_nwt),
                                    (lambda: nc.vector.tensor_tensor(nwt2[:, :], nwt[:, :], rstd0[:, :], ALU.mult), f_nwt2),
                                    (lambda: nc.vector.scalar_tensor_tensor(rstd[:, :], nwt2[:, :], 1.5, rstd0[:, :], ALU.add, ALU.mult), f_rstd)):
                        ins().then_inc(s_, 1)
                        ve.wait_ge(s_, c)
                    nc.vector.scalar_tensor_tensor(nmr[:, :], mv2[:, 1 - c % 2, :, 0], -1.0, rstd[:, :],
                                                   ALU.mult, ALU.mult).then_inc(f_nmr, 1)
                if c < G:
                    nc.vector.tensor_scalar(var[:, :], mv2[:, q, :, 1], EPS_LN, None, ALU.add).then_inc(f_var, 1)

        @block.gpsimd
        def _(pool):
            def scatter(b, par):
                pool.wait_ge(a_rowb, b + 1)
                pool.wait_ge(v_row, b + 1)
                pool.dma_start(x1_all[:, bass.ds(T * b, T), :], rows[:, par, 0, :, 0:D]).then_inc(s_keep[par], 16)
                for k in range(2):
                    for t in range(T):
                        nc.gpsimd.indirect_dma_start(
                            regions, bass.IndirectOffsetOnAxis(ap=pos[:, par, k, t:t + 1], axis=0),
                            rows[:, par, k, t, :], None).then_inc(s_scat[par], 16)

            pool.dma_start(wsp[:, :, :, 0, :].rearrange("p e w h -> p (e w) h"),
                           wts.rearrange("p e w h -> p (e w) h")).then_inc(s_whi, 16)
            with pool.Fori(0, G // 2) as i:
                scatter(2 * i, 0)
                scatter(2 * i + 1, 1)

            last_row = pool.to_reg(2 * TOK - 1)

            def tile_step(t, n, r):
                if not isinstance(t, int) or 0 <= t - 2 < TILES:
                    pool.wait_ge(a_yo, t - 1)
                    pool.sem_inc(g_turn, 1)
                    for j in range(SJ):
                        nc.gpsimd.indirect_dma_start(
                            returned, bass.IndirectOffsetOnAxis(ap=back[:, (r - 2) % RING, j, 0:1].bitcast(I32), axis=0),
                            yo[:, r % 2, j, :], None, bounds_check=last_row, oob_is_err=False
                        ).then_inc(s_ret[(r - 2) % RING], 16)

            tiles(pool, tile_step)
            for r in range(RING):
                pool.wait_ge(s_ret[r], 16 * SJ * len(range(r, TILES, RING)))


def kernel(L0_attn_x, L0_attn_Wq, L0_attn_bq, L0_attn_Wk, L0_attn_bk, L0_attn_Wv, L0_attn_bv, L0_attn_gamma,
           L0_ffn_router_w, L0_ffn_w1, L0_ffn_b1, L0_ffn_w2, L0_ffn_b2):
    import concourse.bacc as _bacc
    from concourse.bass_utils import run_bass_kernel_spmd as _run

    x = np.ascontiguousarray(L0_attn_x).reshape(TOK, D)
    w1T = np.transpose(L0_ffn_w1, (0, 2, 1))
    w2T = np.transpose(np.reshape(L0_ffn_w2, (E, D, HC, P)), (0, 3, 2, 1)).reshape(E, P, H)
    b1c = np.transpose(np.reshape(L0_ffn_b1, (E, HC, P)), (2, 0, 1))
    b2c = np.transpose(L0_ffn_b2, (1, 0))[:, :, None]
    consts = np.zeros((P, K_COLS), np.float32)
    consts[:, K_ID:K_ID + P] = np.eye(P)
    consts[:, K_TRI:K_TRI + P] = np.triu(np.ones((P, P)), 1)
    consts[:, K_REV:K_REV + T * E] = np.tile(E - np.arange(E), T)
    consts[:, K_BASE:K_BASE + E] = REG * np.arange(E)
    consts[:, K_THR:K_T] = np.tile(SLOTS * np.arange(TOK // SLOTS), E)
    consts[:, K_T:K_TS] = np.repeat(np.arange(TILES), E)
    consts[:, K_TS:K_COLS] = SLOTS * np.arange(TILES)
    returns = (np.arange(P)[:, None, None, None] + GC * np.arange(G)[None, :, None, None]
               + TOK * np.arange(2)[None, None, :, None] + P * np.arange(T)[None, None, None, :]).astype(np.int32)
    arrays = {
        "x": x,
        "xT": x.T,
        "wqkT": np.concatenate([np.transpose(L0_attn_Wq), np.transpose(L0_attn_Wk)], axis=1),
        "wvT": np.transpose(L0_attn_Wv),
        "bqk": np.concatenate([L0_attn_bq, L0_attn_bk]),
        "bv": np.reshape(L0_attn_bv, (D, 1)),
        "gamma": L0_attn_gamma,
        "rwT": np.transpose(L0_ffn_router_w),
        "wts": np.stack([np.transpose(w1T, (1, 0, 2)), np.transpose(w2T, (1, 0, 2))], axis=2),
        "bcols": np.concatenate([b1c, b2c], axis=2),
        "consts": consts,
        "returns": returns,
    }
    arrays = {"in_" + k: np.ascontiguousarray(v) for k, v in arrays.items()}
    nc = _bacc.Bacc("TRN2", target_bir_lowering=False, num_devices=1)
    args = [nc.dram_tensor(k, v.shape, mybir.dt.from_np(v.dtype), kind="ExternalInput").ap() for k, v in arrays.items()]
    args.append(nc.dram_tensor("out_0", (TOK, D), F32, kind="ExternalOutput").ap())
    args.append(nc.dram_tensor("regions", ((E + 1) * REG, ROW), F32, kind="Internal").ap())
    args.append(nc.dram_tensor("returned", (2 * TOK, D), F32, kind="Internal").ap())
    moe_layer(nc, *args)
    r = _run(nc, [arrays], core_ids=[0])
    return r.results[0]["out_0"].reshape(B, C, D)
```

```python
from contextlib import ExitStack

import numpy as np

import concourse.bass as bass
from concourse import mybir

P = 128
B, C, D = 16, 256, 128
TOK = B * C
E = 8
H = 4 * D
HC = H // P
NT = TOK // P
GB = 2
T = GB * C // P
G = B // GB
GC = T * P
SLOTS = 512
SJ = SLOTS // P
TILES = (2 * TOK - E) // SLOTS + E
NF = -(-TOK // SLOTS)
REG = TOK + SLOTS
ROW = D + 2
SKIP = 1 << 20
EPS_K = 1e-6
EPS_LN = 1e-5
NEG = -1e30
ACT_GELU = "gelu_apprx_tanh_and_others"
ACT_LN_EXP = "natural_log_exp_and_others"

F32 = mybir.dt.float32
F32R = mybir.dt.float32r
BF16 = mybir.dt.bfloat16
I32 = mybir.dt.int32
ALU = mybir.AluOpType
ACT = mybir.ActivationFunctionType
AX = mybir.AxisListType

K_ID, K_TRI, K_REV, K_BASE = 0, P, 2 * P, 2 * P + T * E
K_THR = K_BASE + E
K_T = K_THR + E * NF
K_TS = K_T + TILES * E
K_COLS = K_TS + TILES
RING = 4


def moe_layer(nc, x, xT, cols, vecs, wts, bcols, consts, returns, out,
              regions, returned):
    with ExitStack() as ctx:
        def sb(name, shape, dt=F32):
            return ctx.enter_context(nc.sbuf_tensor(name, shape, dt))

        def psum(name, shape):
            return ctx.enter_context(nc.psum_tensor(name, shape, F32))

        def sem(name):
            return ctx.enter_context(nc.semaphore(name))

        bank = psum("bank", [P, 8, 512])
        qk_ps = bank[:, 0:2, :]
        vT_ps = bank[:, 2, :]
        kq_ps = bank[:, 3, 0:GB * D].rearrange("p (b n) -> p b n", b=GB)
        qss_ps = bank[:, 4, 0:GB * D].rearrange("p (b n) -> p b n", b=GB)
        kss_ps = bank[:, 4, GB * D:GB * D + GB]
        ss_ps = bank[:, 4, 0:GB * D + GB]
        att_ps = bank[:, 5, :]
        x1T_ps = bank[:, 6, :]
        lg_ps = bank[:, 7, 0:T * E].rearrange("p (t e) -> p t e", t=T)
        rk_ps = bank[:, 7, 64:64 + T * E].rearrange("p (t e) -> p t e", t=T)
        tot_ps = bank[:, 7, 128:128 + E]

        k_sb = sb("k_sb", [P, K_COLS])
        ident = k_sb[:, K_ID:K_ID + P]
        rev = k_sb[:, K_REV:K_REV + T * E].rearrange("p (t e) -> p t e", t=T)
        ret_sb = sb("ret_sb", [P, G, 2, T], I32)
        cols_sb = sb("cols_sb", [P, 3 * D + E + 1])
        wqk_sb, wv_sb = cols_sb[:, 0:2 * D], cols_sb[:, 2 * D:3 * D]
        rw_sb, bv_sb = cols_sb[:, 3 * D:3 * D + E], cols_sb[:, 3 * D + E:3 * D + E + 1]
        vecs_sb = sb("vecs_sb", [P, 2 * D + 1])
        bqk_sb, gam_sb = vecs_sb[:, 0:2 * D], vecs_sb[:, 2 * D:2 * D + 1]
        gam2 = sb("gam2", [P, 1])
        bcol_sb = sb("bcol_sb", [P, E, HC + 1])
        ones = sb("ones", [P, P])
        epsm = sb("epsm", [P, P])
        width = sb("width", [P, 1])
        tri16 = sb("tri16", [P, P], BF16)
        ones16 = sb("ones16", [P, P], BF16)

        x_sb = sb("x_sb", [P, 2, T * D])
        xT_sb = sb("xT_sb", [P, 2, GC])
        work = sb("work", [P, 2, T * 2 * D])
        qk = work[:, 0, :].rearrange("p (t n) -> p t n", t=T)
        qk2 = work[:, 1, :].rearrange("p (t n) -> p t n", t=T)
        x1s = sb("x1s", [P, T, D])
        vT = sb("vT", [P, GC])
        lnss = sb("lnss", [P, GB * D + GB])
        inv = sb("inv", [P, GB * D + GB])
        invq = inv[:, 0:GB * D].rearrange("p (b n) -> p b n", b=GB)
        invk = inv[:, GB * D:GB * D + GB]
        g1 = sb("g1", [P, GB, D])
        den = sb("den", [P, GB, D])
        tail = sb("tail", [P, GB, D])
        lnd = sb("lnd", [P, GB, D])
        gq = sb("gq", [P, GB, D])
        mm = sb("mm", [P, GB, D])
        z = sb("z", [P, T, D])
        st6 = sb("st6", [P, T, 6])
        mv = sb("mv", [P, T, 2])
        mv2 = sb("mv2", [P, 2, T, 2])
        var = sb("var", [P, T])
        lnv = sb("lnv", [P, T])
        rstd0 = sb("rstd0", [P, T])
        nwt = sb("nwt", [P, T])
        nwt2 = sb("nwt2", [P, T])
        rstd = sb("rstd", [P, T])
        nmr = sb("nmr", [P, T])
        rows = sb("rows", [P, 2, 2, T, ROW])
        rows_i = rows[:, :, :, :, :].bitcast(I32)
        x1T = sb("x1T", [P, GC])
        x1_all = sb("x1_all", [P, NT, D])

        m1 = sb("m1", [P, T])
        dl = sb("dl", [P, T, E])
        key1 = sb("key1", [P, T, E])
        km1 = sb("km1", [P, T])
        oh12 = sb("oh12", [P, 2, T, E])
        dl2 = sb("dl2", [P, T, E])
        m2 = sb("m2", [P, T])
        eq2 = sb("eq2", [P, T, E])
        key2 = sb("key2", [P, T, E])
        km2 = sb("km2", [P, T])
        oh16 = sb("oh16", [P, T, E], BF16)
        base = sb("base", [P, 2, E])
        place = sb("place", [P, T, E])
        sel = sb("sel", [P, 2, T, E])
        pos = sb("pos", [P, 2, 2, T], I32)
        ex = sb("ex", [P, T, E])
        ex2 = sb("ex2", [P, T])
        zs = sb("zs", [P, T])
        rz = sb("rz", [P, T])
        p2 = sb("p2", [P, T])
        ps_ = sb("ps_", [P, T])
        rs = sb("rs", [P, T])

        thr = k_sb[:, K_THR:K_THR + E * NF].rearrange("p (e n) -> p e n", e=E)
        tno = k_sb[:, K_T:K_T + TILES * E].rearrange("p (t e) -> p t e", t=TILES)
        tsl = k_sb[:, K_TS:K_TS + TILES]
        cnt = sb("cnt", [P, E])
        over = sb("over", [P, E, NF])
        ntile = sb("ntile", [P, E])
        cum = sb("cum", [P, E])
        past = sb("past", [P, TILES, E])
        pastn = sb("pastn", [P, TILES, E])
        tex = sb("tex", [P, TILES])
        tst = sb("tst", [P, TILES])
        toff = sb("toff", [P, TILES])
        trow = sb("trow", [P, TILES])
        row_i = sb("row_i", [P, TILES], I32)
        exp_i = sb("exp_i", [P, TILES], I32)
        pad_i = sb("pad_i", [P, E], I32)

        h_ps = bank[:, 0:HC, 0:SLOTS]
        xg_ps = bank[:, 4, 0:SLOTS]
        y_ps = bank[:, 5, 0:SLOTS]
        yt_ps = bank[:, 6, 0:SLOTS]
        pad_sb = sb("pad_sb", [P, SJ, ROW])
        wraw = sb("wraw", [P, 2, H])
        wsp = sb("wsp", [P, E, 2, 2, H], F32R)
        w1st = sb("w1st", [P, 2, 2, H], F32R)
        w2st = sb("w2st", [P, 2, 2, H], F32R)
        bst = sb("bst", [P, RING, HC + 1])
        xg = sb("xg", [P, RING, SJ, ROW])
        xh = sb("xh", [P, SLOTS], F32R)
        xl = sb("xl", [P, SLOTS], F32R)
        h_sb = work[:, :, :].rearrange("p a (m s) -> p (a m) s", m=HC // 2)[:, :, 0:SLOTS]
        hh = sb("hh", [P, 2, HC, SLOTS], F32R)
        hl = sb("hl", [P, 2, HC, SLOTS], F32R)
        y_sb = sb("y_sb", [P, SLOTS])
        yo = sb("yo", [P, 2, SJ, D])
        back = sb("back", [P, RING, SJ, 2])

        s_cols, s_vecs, s_const, s_set = [sem(n) for n in ("s_cols", "s_vecs", "s_const", "s_set")]
        s_x = [sem("s_x0"), sem("s_x1")]
        s_xT = [sem("s_xT0"), sem("s_xT1")]
        (s_qk, s_vT, s_kq, s_stat, s_den, s_att, s_xt, s_lg, s_rk) = [sem("pe_" + n) for n in (
            "qk", "vT", "kq", "stat", "den", "att", "xt", "lg", "rk")]
        (a_lnv, a_rstd, a_x1, a_vT, a_sq, a_lnss, a_inv, a_x1T, a_g1, a_rows, a_ex, a_lnd, a_tail) = [
            sem("act_" + n) for n in ("lnv", "rstd", "x1", "vT", "sq", "lnss", "inv", "x1T", "g1", "rows", "ex",
                                      "lnd", "tail")]
        (v_z, v_st, v_mv, v_var, v_nwt, v_nwt2, v_rstd, v_nmr, v_qk, v_den, v_gq, v_ndr, v_tail, v_mm, v_m1,
         v_dl, v_key1, v_km1, v_oh1, v_dl2, v_m2, v_eq2, v_key2, v_km2, v_oh2, v_oh, v_place,
         v_base, v_sel, v_zs, v_rz, v_p2, v_ps, v_rs, v_row) = [sem("dve_" + n) for n in (
            "z", "st", "mv", "var", "nwt", "nwt2", "rstd", "nmr", "qk", "den", "gq", "ndr", "tail", "mm", "m1",
            "dl", "key1", "km1", "oh1", "dl2", "m2", "eq2", "key2", "km2", "oh2", "oh", "place",
            "base", "sel", "zs", "rz", "p2", "ps", "rs", "row")]
        s_scat = [sem("s_scat0"), sem("s_scat1")]
        g_free = sem("pool_rows_free")
        s_keep = sem("s_keep")
        SCAT = 16 * 2 * T
        s_done = [sem("s_done0"), sem("s_done1")]
        s_pad0 = sem("s_pad0")
        s_wraw = [sem("s_wraw0"), sem("s_wraw1")]
        s_whi, s_wlo = sem("s_whi"), sem("s_wlo")
        v_tab = sem("dve_table")
        v_const = sem("dve_const")
        g_turn = sem("pool_turn")
        v_chain = sem("dve_chain")
        s_pads = sem("s_pads")
        s_tile = [sem(f"s_tile{r}") for r in range(RING)]
        s_bst = [sem(f"s_bst{r}") for r in range(RING)]
        s_w1 = [sem("s_w1st0"), sem("s_w1st1")]
        s_w2 = [sem("s_w2st0"), sem("s_w2st1")]
        p_xg, p_h, p_y, p_yt = [sem("pe_" + n) for n in ("xg", "h", "y", "ytr")]
        a_h, a_y, a_yo = [sem("act_" + n) for n in ("h", "y", "yo")]
        v_pad, v_xh, v_xl, v_hh, v_hl, v_back = [sem("dve_" + n) for n in ("pad", "xh", "xl", "hh", "hl", "back")]
        s_ret = [sem(f"s_ret{r}") for r in range(RING)]
        s_y1 = [sem("s_y10"), sem("s_y11")]
        s_y2 = [sem("s_y20"), sem("s_y21")]
        (f_z1, f_z, f_st, f_mv, f_var, f_nwt, f_nwt2, f_rstd, f_nmr) = [sem("fin_" + n) for n in (
            "z1", "z", "st", "mv", "var", "nwt", "nwt2", "rstd", "nmr")]
        SET, CONST = 5, 16 * 3
        g_lnv, g_rstd, g_out = [sem("fina_" + n) for n in ("lnv", "rstd", "out")]

        block = ctx.enter_context(nc.Block())

        def steps(eng, step):
            step(0, None, None, 0)
            step(1, 0, None, 1)
            step(2, 1, 0, 0)
            with eng.Fori(1, G // 2 - 1) as i:
                step(2 * i + 1, 2 * i, 2 * i - 1, 1)
                step(2 * i + 2, 2 * i + 1, 2 * i, 0)
            step(G - 1, G - 2, G - 3, 1)
            step(None, G - 1, G - 2, 0)
            step(None, None, G - 1, 1)

        def loaded(g, par):
            return 16 * (g // 2 + 1) if isinstance(g, int) else 8 * (g + 2 - par)

        def after(eng, s, n):
            if not isinstance(n, int) or n > 0:
                eng.wait_ge(s, n)

        def tiles(eng, step):
            last = (TILES - 3) // RING
            for t in range(RING + 1):
                step(t, t // RING, t % RING)
            with eng.Fori(1, last) as i:
                for k in range(1, RING + 1):
                    step(RING * i + k, i + k // RING, k % RING)
            for t in range(RING * last + 1, TILES + 2):
                step(t, t // RING, t % RING)

        def within(t):
            return not isinstance(t, int) or 0 <= t < TILES

        @block.sync
        def _(sp):
            x_groups = x.rearrange("(g t p) d -> g p t d", t=T, p=P)
            xT_groups = xT.rearrange("d (g n) -> g d n", n=GC)

            def load_xT(g, par):
                src = xT_groups[g] if isinstance(g, int) else xT_groups[bass.ds(g, 1)].rearrange("o d n -> d (o n)")
                sp.dma_start(xT_sb[:, par, :], src).then_inc(s_xT[par], 16)

            def load_x(g, par):
                src = x_groups[g] if isinstance(g, int) else x_groups[bass.ds(g, 1)].rearrange("o p t d -> p (o t) d")
                sp.dma_start(x_sb[:, par, :].rearrange("p (t d) -> p t d", t=T), src).then_inc(s_x[par], 16)

            def load_step(s, par):
                if not isinstance(s, int) or s + 2 < G:
                    sp.wait_ge(s_vT, s + 1)
                    load_xT(s + 2, par)
                if not isinstance(s, int) or s + 1 < G:
                    sp.wait_ge(v_z, s)
                    load_x(s + 1, 1 - par)
                for w in range(2):
                    after(sp, s_wlo, 2 * s - 3 + w)
                    src = wts[:, s - 1, w, :] if isinstance(s, int) else \
                        wts[:, bass.ds(s - 1, 1), w, :].rearrange("p o h -> p (o h)")
                    sp.dma_start(wraw[:, w, :], src).then_inc(s_wraw[w], 16)
                sp.wait_ge(a_x1, s)
                dst = x1_all[:, T * (s - 1):T * s, :] if isinstance(s, int) else x1_all[:, bass.ds(T * (s - 1), T), :]
                sp.dma_start(dst, x1s[:, :, :]).then_inc(s_keep, 16)

            load_xT(0, 0)
            sp.dma_start(cols_sb[:, :], cols).then_inc(s_cols, 16)
            sp.dma_start(vecs_sb[:, :], vecs.partition_broadcast(P)).then_inc(s_vecs, 16)
            load_xT(1, 1)
            load_x(0, 0)
            load_x(1, 1)
            for dst, src in ((k_sb[:, :], consts), (ret_sb[:, :, :, :], returns), (bcol_sb[:, :, :], bcols)):
                sp.dma_start(dst, src).then_inc(s_const, 16)
            sp.wait_ge(s_vT, 1)
            load_xT(2, 0)
            load_step(1, 1)
            sp.wait_ge(v_pad, 2)
            sp.dma_start(regions[E * REG:E * REG + SLOTS, :].rearrange("(p j) c -> p j c", j=SJ),
                         pad_sb[:, :, :]).then_inc(s_pad0, 16)
            with sp.Fori(1, G // 2 - 1) as i:
                load_step(2 * i, 0)
                load_step(2 * i + 1, 1)
            for s in range(G - 2, G + 1):
                load_step(s, s % 2)
            sp.wait_ge(v_tab, 3)
            for e in range(E):
                row = sp.value_load(pad_i[0:1, e:e + 1], min_val=e * REG, max_val=e * REG + TOK)
                sp.dma_start(regions[bass.ds(row, SLOTS), :].rearrange("(p j) c -> p j c", j=SJ),
                             pad_sb[:, :, :]).then_inc(s_pads, 16)
            for q in range(2):
                sp.wait_ge(s_scat[q], SCAT * (G // 2))
            sp.wait_ge(s_keep, 16 * G)
            sp.wait_ge(s_pads, 16 * E)
            sp.wait_ge(s_pad0, 16)
            sp.wait_ge(s_wlo, 2 * E)

            def load_tile(t, n, r):
                after(sp, v_back, t - RING + 1)
                row = sp.value_load(row_i[0:1, t:t + 1] if isinstance(t, int) else row_i[0:1, bass.ds(t, 1)],
                                    min_val=0, max_val=E * REG)
                sp.dma_start(xg[:, r, :, :], regions[bass.ds(row, SLOTS), :].rearrange("(p j) c -> p j c", j=SJ)
                             ).then_inc(s_tile[r], 16)

            def expert(t):
                return sp.value_load(exp_i[0:1, t:t + 1] if isinstance(t, int) else exp_i[0:1, bass.ds(t, 1)],
                                     min_val=0, max_val=E - 1)

            def load_first(t, e, r):
                after(sp, p_h, HC * (t - 1))
                sp.dma_start(w1st[:, r % 2, :, :].bitcast(F32),
                             wsp[:, bass.ds(e, 1), 0, :, :].bitcast(F32).rearrange("p o a h -> p (o a) h")
                             ).then_inc(s_w1[r % 2], 16)
                after(sp, a_y, t - RING + 1)
                sp.dma_start(bst[:, r, :], bcol_sb[:, bass.ds(e, 1), :].rearrange("p o a -> p (o a)")
                             ).then_inc(s_bst[r], 16)

            def load_step(t, n, r):
                if isinstance(t, int) and t == 0:
                    load_tile(0, 0, 0)
                    load_first(0, expert(0), 0)
                    load_tile(1, 0, 1)
                if within(t):
                    e = expert(t)
                if within(t) and (not isinstance(t, int) or t + 2 < TILES):
                    load_tile(t + 2, None, (r + 2) % RING)
                if within(t) and (not isinstance(t, int) or t + 1 < TILES):
                    load_first(t + 1, expert(t + 1), (r + 1) % RING)
                if within(t):
                    after(sp, p_y, t - 1)
                    sp.dma_start(w2st[:, r % 2, :, :].bitcast(F32),
                                 wsp[:, bass.ds(e, 1), 1, :, :].bitcast(F32).rearrange("p o a h -> p (o a) h")
                                 ).then_inc(s_w2[r % 2], 16)

            tiles(sp, load_step)

            for r in range(RING):
                sp.wait_ge(s_ret[r], 16 * SJ * len(range(r, TILES, RING)))
            ret = returned.rearrange("(k g t p) d -> k g p t d", k=2, t=T, p=P)
            outg = out.rearrange("(g t p) d -> g p t d", t=T, p=P)
            for c in range(G + 2):
                q = c % 2
                if c < G:
                    after(sp, f_z, c - 1)
                    sp.dma_start(x_sb[:, q, :].rearrange("p (t d) -> p t d", t=T), ret[0, c]).then_inc(s_y1[q], 16)
                    sp.dma_start(xT_sb[:, q, :].rearrange("p (t d) -> p t d", t=T), ret[1, c]).then_inc(s_y2[q], 16)
                if c >= 2:
                    sp.wait_ge(g_out, c - 1)
                    sp.dma_start(outg[c - 2], x1_all[:, T * (c - 2):T * (c - 1), :]).then_inc(s_done[q], 16)
            for q in range(2):
                sp.wait_ge(s_done[q], 16 * (G // 2))

        @block.tensor
        def _(pe):
            def project_qk(g, par, b):
                for t in range(b * C // P, (b + 1) * C // P):
                    last = nc.tensor.matmul(qk_ps[:, b, t % 2 * 2 * D:(t % 2 + 1) * 2 * D],
                                            xT_sb[:, par, t * P:(t + 1) * P], wqk_sb, start=True, stop=True)
                last.then_inc(s_qk, 1)

            def project_v(g, par):
                after(pe, a_vT, g)
                nc.tensor.matmul(vT_ps, wv_sb, xT_sb[:, par, :], start=True, stop=True).then_inc(s_vT, 1)

            def step(f, b, c, par):
                if c is not None:
                    pe.wait_ge(a_x1, c + 1)
                    after(pe, a_x1T, c)
                    for t in range(T):
                        last = nc.tensor.transpose(x1T_ps[:, t * P:(t + 1) * P], x1s[:, t, :], ident)
                    last.then_inc(s_xt, 1)
                if b is not None:
                    pe.wait_ge(v_mm, b + 1)
                    after(pe, v_z, b)
                    for t in range(T):
                        last = nc.tensor.matmul(att_ps[:, t * D:(t + 1) * D], vT[:, t * P:(t + 1) * P],
                                                mm[:, t * P // C, :], start=True, stop=True)
                    last.then_inc(s_att, 1)
                if c is not None:
                    pe.wait_ge(a_x1T, c + 1)
                    after(pe, v_base, c)
                    for t in range(T):
                        last = nc.tensor.matmul(lg_ps[:, t, :], x1T[:, t * P:(t + 1) * P], rw_sb, start=True, stop=True)
                    last.then_inc(s_lg, 1)
                if f is not None:
                    pe.wait_ge(v_qk, f + 1)
                    after(pe, v_den, f)
                    for t in range(T):
                        last = nc.tensor.matmul(kq_ps[:, t * P // C, :], qk[:, t, D:2 * D], qk[:, t, 0:D],
                                                start=t * P % C == 0, stop=(t + 1) * P % C == 0)
                    last.then_inc(s_kq, 1)
                    pe.wait_ge(a_sq, f + 1)
                    after(pe, a_lnss, f)
                    for t in range(T):
                        nc.tensor.matmul(qss_ps[:, t * P // C, :], ones[:, :], qk2[:, t, 0:D],
                                         start=t * P % C == 0, stop=(t + 1) * P % C == 0)
                    for t in range(T):
                        b0 = t * P // C
                        last = nc.tensor.matmul(kss_ps[:, b0:b0 + 1], qk2[:, t, D:2 * D], ones[:, 0:1],
                                                start=t * P % C == 0, stop=(t + 1) * P % C == 0)
                    last.then_inc(s_stat, 1)
                more = f is not None and (not isinstance(f, int) or f + 1 < G)
                if more:
                    pe.wait_ge(s_xT[1 - par], loaded(f + 1, 1 - par))
                    project_qk(f + 1, 1 - par, 0)
                if f is not None:
                    pe.wait_ge(a_g1, f + 1)
                    for q in range(GB):
                        for t in range(q * C // P, (q + 1) * C // P):
                            nc.tensor.matmul(kq_ps[:, q, :], epsm[:, :], qk[:, t, 0:D],
                                             start=t * P % C == 0, stop=False)
                        last = nc.tensor.matmul(kq_ps[:, q, :], ones[:, :], g1[:, q, :], start=False, stop=True)
                    last.then_inc(s_den, 1)
                if c is not None:
                    pe.wait_ge(v_oh, c + 1)
                    if isinstance(c, int) and c == 0:
                        pe.wait_ge(v_const, 2)
                    nc.tensor.matmul(rk_ps[:, :, :], tri16[:, :], oh16[:, :, :], start=True, stop=True)
                    for t in range(T - 1):
                        for u in range(t + 1, T):
                            nc.tensor.matmul(rk_ps[:, u, :], ones16[:, :], oh16[:, t, :], start=False,
                                             stop=True, skip_group_check=True)
                    for t in range(T):
                        last = nc.tensor.matmul(tot_ps, ones16[:, :], oh16[:, t, :], start=t == 0, stop=t == T - 1,
                                                skip_group_check=True)
                    last.then_inc(s_rk, 1)
                if more:
                    project_qk(f + 1, 1 - par, 1)
                    project_v(f + 1, 1 - par)

            pe.wait_ge(s_xT[0], 16)
            pe.wait_ge(s_cols, 16)
            for b in range(GB):
                project_qk(0, 0, b)
            project_v(0, 0)
            pe.wait_ge(s_set, SET)
            pe.wait_ge(s_const, CONST)
            steps(pe, step)

            def tile_step(t, n, r):
                par = r % 2
                int_t = isinstance(t, int)

                def transposed(t, n, r):
                    pe.wait_ge(s_tile[r], 16 * (n + 1))
                    after(pe, v_xl, t)
                    for j in range(SJ):
                        last = nc.tensor.transpose(xg_ps[:, j * P:(j + 1) * P], xg[:, r, j, 0:D], ident)
                    last.then_inc(p_xg, 1)

                if int_t and t == 0:
                    pe.wait_ge(v_base, G)
                    pe.wait_ge(a_x1T, G)
                    pe.wait_ge(v_z, G)
                    pe.wait_ge(v_mm, G)
                    transposed(0, 0, 0)
                if within(t):
                    pe.wait_ge(s_w1[par], 16 * (t // 2 + 1) if int_t else 8 * (t - par) + 16)
                    pe.wait_ge(v_xl, t + 1)
                    for m in range(HC):
                        cols = slice(m * P, (m + 1) * P)
                        after(pe, a_h, HC * (t - 1) + m + 1)
                        nc.tensor.matmul(h_ps[:, m, :], w1st[:, par, 0, cols], xh[:, :], start=True, stop=False)
                        nc.tensor.matmul(h_ps[:, m, :], w1st[:, par, 0, cols], xl[:, :], start=False, stop=False)
                        nc.tensor.matmul(h_ps[:, m, :], w1st[:, par, 1, cols], xh[:, :], start=False, stop=True
                                         ).then_inc(p_h, 1)
                if within(t) and (not int_t or t + 1 < TILES):
                    transposed(t + 1, n + (r == RING - 1), (r + 1) % RING)
                if (not int_t or t >= 2) and (not int_t or t - 2 < TILES):
                    pe.wait_ge(a_y, t - 1)
                    after(pe, a_yo, t - 2)
                    for j in range(SJ):
                        last = nc.tensor.transpose(yt_ps[:, j * P:(j + 1) * P], y_sb[:, j * P:(j + 1) * P], ident)
                    last.then_inc(p_yt, 1)
                if (not int_t or 1 <= t <= TILES):
                    pe.wait_ge(s_w2[1 - par], 16 * ((t - 1) // 2 + 1) if int_t else 8 * (t + par))
                    after(pe, a_y, t - 1)
                    for m in range(HC):
                        cols = slice(m * P, (m + 1) * P)
                        pe.wait_ge(v_hl, HC * (t - 1) + m + 1)
                        nc.tensor.matmul(y_ps, w2st[:, 1 - par, 0, cols], hh[:, 1 - par, m, :], start=m == 0, stop=False)
                        nc.tensor.matmul(y_ps, w2st[:, 1 - par, 0, cols], hl[:, 1 - par, m, :], start=False, stop=False)
                        last = nc.tensor.matmul(y_ps, w2st[:, 1 - par, 1, cols], hh[:, 1 - par, m, :], start=False,
                                                stop=m == HC - 1)
                    last.then_inc(p_y, 1)

            tiles(pe, tile_step)

        @block.scalar
        def _(act):
            def step(f, b, c, par):
                if c is not None:
                    act.wait_ge(s_xt, c + 1)
                    after(act, s_lg, c)
                    nc.scalar.copy(x1T[:, :], x1T_ps).then_inc(a_x1T, 1)
                if f is not None:
                    act.wait_ge(s_vT, f + 1)
                    after(act, s_att, f)
                    nc.scalar.activation(vT[:, :], vT_ps, ACT.Identity, bias=bv_sb).then_inc(a_vT, 1)
                    act.wait_ge(v_qk, f + 1)
                    after(act, s_stat, f)
                    nc.scalar.activation(qk2, qk, ACT.Square).then_inc(a_sq, 1)
                if c is not None:
                    act.wait_ge(g_free, c + 1)
                    for k in range(2):
                        last = nc.scalar.copy(rows[:, par, k, :, 0:D], x1s[:, :, :])
                    last.then_inc(a_rows, 1)
                if f is not None:
                    act.wait_ge(s_stat, f + 1)
                    nc.scalar.activation(lnss[:, :], ss_ps, ACT.Ln).then_inc(a_lnss, 1)
                if b is not None:
                    act.wait_ge(v_var, b + 1)
                    nc.scalar.activation(lnv[:, :], var[:, :], ACT.Ln).then_inc(a_lnv, 1)
                if f is not None:
                    act.wait_ge(a_lnss, f + 1)
                    after(act, v_mm, f)
                    nc.scalar.activation(inv[:, :], lnss[:, :], ACT.Exp, scale=-0.5).then_inc(a_inv, 1)
                if b is not None:
                    act.wait_ge(a_lnv, b + 1)
                    after(act, v_rstd, b)
                    nc.scalar.activation(rstd0[:, :], lnv[:, :], ACT.Exp, scale=-0.5).then_inc(a_rstd, 1)
                if f is not None:
                    act.wait_ge(s_kq, f + 1)
                    act.wait_ge(a_inv, f + 1)
                    after(act, v_gq, f)
                    after(act, s_den, f)
                    for q in range(GB):
                        last = nc.scalar.activation(g1[:, q, :], kq_ps[:, q, :], ACT.Copy, scale=invk[:, q:q + 1])
                    last.then_inc(a_g1, 1)
                if c is not None:
                    act.wait_ge(v_m2, c + 1)
                    after(act, v_p2, c)
                    nc.scalar.activation(ex[:, :, :], dl[:, :, :], ACT.Exp)
                    nc.scalar.activation(ex2[:, :], m2[:, :], ACT.Exp).then_inc(a_ex, 1)
                if f is not None:
                    act.wait_ge(v_den, f + 1)
                    nc.scalar.activation(lnd[:, :, :], den[:, :, :], ACT.Ln, bias=width[:, 0:1]).then_inc(a_lnd, 1)
                    act.wait_ge(a_lnd, f + 1)
                    after(act, v_mm, f)
                    nc.scalar.activation(tail[:, :, :], lnd[:, :, :], ACT.Exp, scale=-1.0).then_inc(a_tail, 1)
                if b is not None:
                    act.wait_ge(v_nmr, b + 1)
                    after(act, s_xt, b)
                    after(act, a_rows, b)
                    after(act, s_keep, 16 * b)
                    for t in range(T):
                        last = nc.scalar.activation(x1s[:, t, :], z[:, t, :], ACT.Identity,
                                                    bias=nmr[:, t:t + 1], scale=rstd[:, t:t + 1])
                    last.then_inc(a_x1, 1)

            act.wait_ge(s_cols, 16)
            act.wait_ge(s_set, SET)
            act.preload_act_table_set(ACT_LN_EXP)
            steps(act, step)
            act.preload_act_table_set(ACT_GELU)

            def tile_step(t, n, r):
                int_t = isinstance(t, int)
                if (not int_t or 1 <= t - 1 <= TILES):
                    act.wait_ge(p_y, t - 1)
                    after(act, p_yt, t - 2)
                    nc.scalar.activation(y_sb[:, :], y_ps, ACT.Identity, bias=bst[:, (r - 2) % RING, HC:HC + 1]
                                         ).then_inc(a_y, 1)
                if within(t):
                    act.wait_ge(s_bst[r], 16 * (n + 1))
                    for m in range(HC):
                        act.wait_ge(p_h, HC * t + m + 1)
                        after(act, v_hl, HC * (t - 1) + m + 1)
                        nc.scalar.activation(h_sb[:, m, :], h_ps[:, m, :], ACT.Gelu_apprx_tanh, bias=bst[:, r, m:m + 1]
                                             ).then_inc(a_h, 1)
                if (not int_t or 0 <= t - 2 < TILES):
                    act.wait_ge(p_yt, t - 1)
                    act.wait_ge(v_back, t - 1)
                    if not int_t:
                        act.wait_ge(s_ret[r % 4], 16 * SJ * n)
                    elif t >= 4:
                        act.wait_ge(s_ret[r % 4], 16 * SJ * (t // 4))
                    for j in range(SJ):
                        last = nc.scalar.activation(yo[:, r % 2, j, :], yt_ps[:, j * P:(j + 1) * P], ACT.Copy,
                                                    scale=back[:, (r - 2) % RING, j, 1:2])
                    last.then_inc(a_yo, 1)

            tiles(act, tile_step)
            act.preload_act_table_set(ACT_LN_EXP)
            for c in range(G + 1):
                if c < G:
                    act.wait_ge(f_var, c + 1)
                    nc.scalar.activation(lnv[:, :], var[:, :], ACT.Ln).then_inc(g_lnv, 1)
                    act.wait_ge(g_lnv, c + 1)
                    after(act, f_rstd, c)
                    nc.scalar.activation(rstd0[:, :], lnv[:, :], ACT.Exp, scale=-0.5).then_inc(g_rstd, 1)
                if c >= 1:
                    act.wait_ge(f_nmr, c)
                    for t in range(T):
                        u = T * (c - 1) + t
                        last = nc.scalar.activation(x1_all[:, u, :], x1_all[:, u, :], ACT.Identity,
                                                    bias=nmr[:, t:t + 1], scale=rstd[:, t:t + 1])
                    last.then_inc(g_out, 1)

        @block.vector
        def _(ve):
            nc.vector.memset(ones[:, :], 1.0).then_inc(s_set, 1)
            nc.vector.memset(epsm[:, :], EPS_K).then_inc(s_set, 1)
            nc.vector.memset(ones16[:, :], 1.0).then_inc(s_set, 1)
            nc.vector.memset(width[:, :], float(D)).then_inc(s_set, 1)
            nc.vector.memset(pad_sb[:, :, :], 0.0).then_inc(v_pad, 1)
            ve.wait_ge(v_pad, 1)
            nc.vector.memset(pad_sb[:, :, D:D + 1].bitcast(I32), SKIP).then_inc(v_pad, 1)
            ve.wait_ge(s_vecs, 16)
            nc.vector.tensor_scalar(gam2[:, :], gam_sb, -0.5, None, ALU.mult).then_inc(s_set, 1)

            def wide(a):
                return a.unsqueeze(2).to_broadcast([P, T, E])

            def step(f, b, c, par):
                F, B_, R = f is not None, b is not None, c is not None

                def done(ins, s, g):
                    ins.then_inc(s, 1)
                    ve.wait_ge(s, g + 1)

                if F:
                    ve.wait_ge(s_qk, GB * f + GB)
                    after(ve, s_den, f)
                    after(ve, a_sq, f)
                    for s in range(GB):
                        last = nc.vector.tensor_tensor(
                            qk[:, 2 * s:2 * s + 2, :], qk_ps[:, s, :].rearrange("p (t n) -> p t n", t=2),
                            bqk_sb.unsqueeze(1).to_broadcast([P, 2, 2 * D]), ALU.add)
                    last.then_inc(v_qk, 1)
                if B_:
                    ve.wait_ge(s_att, b + 1)
                    ve.wait_ge(s_x[1 - par], loaded(b, 1 - par))
                    after(ve, a_x1, b)
                    nc.vector.scalar_tensor_tensor(z[:, :, :].rearrange("p t d -> p (t d)"), att_ps, gam2[:, 0:1],
                                                   x_sb[:, 1 - par, :], ALU.mult, ALU.add).then_inc(v_z, 1)
                if R:
                    ve.wait_ge(s_lg, c + 1)
                    nc.vector.tensor_reduce(m1[:, :], lg_ps[:, :, :], AX.X, ALU.max).then_inc(v_m1, 1)
                if B_:
                    ve.wait_ge(v_z, b + 1)
                    for t in range(T // 2):
                        nc.vector.bn_stats(st6[:, t, :], z[:, t, :])
                if R:
                    ve.wait_ge(v_m1, c + 1)
                    after(ve, a_ex, c)
                    nc.vector.tensor_tensor(dl[:, :, :], lg_ps[:, :, :], wide(m1[:, :]), ALU.subtract).then_inc(v_dl, 1)
                if B_:
                    for t in range(T // 2, T):
                        last = nc.vector.bn_stats(st6[:, t, :], z[:, t, :])
                    last.then_inc(v_st, 1)
                if R:
                    ve.wait_ge(v_dl, c + 1)
                    nc.vector.scalar_tensor_tensor(key1[:, :, :], dl[:, :, :], 0.0, rev, ALU.is_equal, ALU.mult
                                                   ).then_inc(v_key1, 1)
                    ve.wait_ge(g_free, c + 1)
                    src = ret_sb[:, c] if isinstance(c, int) else \
                        ret_sb[:, bass.ds(c, 1)].rearrange("p o k t -> p (o k) t")
                    nc.vector.tensor_copy(rows_i[:, par, :, :, D], src)
                    if B_:
                        ve.wait_ge(v_st, b + 1)
                    ve.wait_ge(v_key1, c + 1)
                    nc.vector.tensor_reduce(km1[:, :], key1[:, :, :], AX.X, ALU.max).then_inc(v_km1, 1)
                if B_:
                    if not R:
                        ve.wait_ge(v_st, b + 1)
                    for t in range(T):
                        last = nc.vector.bn_aggr(mv[:, t, :], st6[:, t, :])
                    last.then_inc(v_mv, 1)
                if R:
                    ve.wait_ge(v_km1, c + 1)
                    nc.vector.tensor_tensor(oh12[:, 0, :, :], rev, wide(km1[:, :]), ALU.is_equal).then_inc(v_oh1, 1)
                if B_:
                    ve.wait_ge(v_mv, b + 1)
                    nc.vector.tensor_scalar(var[:, :], mv[:, :, 1], EPS_LN / 4, None, ALU.add).then_inc(v_var, 1)
                if R:
                    ve.wait_ge(v_oh1, c + 1)
                    nc.vector.scalar_tensor_tensor(dl2[:, :, :], oh12[:, 0, :, :], NEG, dl[:, :, :], ALU.mult, ALU.add
                                                   ).then_inc(v_dl2, 1)
                    low_half(c, 0)
                    ve.wait_ge(v_dl2, c + 1)
                    done(nc.vector.tensor_reduce(m2[:, :], dl2[:, :, :], AX.X, ALU.max), v_m2, c)
                    done(nc.vector.tensor_tensor(eq2[:, :, :], dl2[:, :, :], wide(m2[:, :]), ALU.is_equal), v_eq2, c)
                    nc.vector.tensor_tensor(key2[:, :, :], eq2[:, :, :], rev, ALU.mult).then_inc(v_key2, 1)
                if B_:
                    ve.wait_ge(a_rstd, b + 1)
                    ve.wait_ge(v_var, b + 1)
                    nc.vector.scalar_tensor_tensor(nwt[:, :], var[:, :], -0.5, rstd0[:, :], ALU.mult, ALU.mult
                                                   ).then_inc(v_nwt, 1)
                if R:
                    ve.wait_ge(v_key2, c + 1)
                    nc.vector.tensor_reduce(km2[:, :], key2[:, :, :], AX.X, ALU.max).then_inc(v_km2, 1)
                if B_:
                    ve.wait_ge(v_nwt, b + 1)
                    nc.vector.tensor_tensor(nwt2[:, :], nwt[:, :], rstd0[:, :], ALU.mult).then_inc(v_nwt2, 1)
                if R:
                    ve.wait_ge(v_km2, c + 1)
                    nc.vector.tensor_tensor(oh12[:, 1, :, :], rev, wide(km2[:, :]), ALU.is_equal).then_inc(v_oh2, 1)
                if B_:
                    ve.wait_ge(v_nwt2, b + 1)
                    nc.vector.scalar_tensor_tensor(rstd[:, :], nwt2[:, :], 1.5, rstd0[:, :], ALU.add, ALU.mult
                                                   ).then_inc(v_rstd, 1)
                if R:
                    ve.wait_ge(v_oh2, c + 1)
                    after(ve, s_rk, c)
                    nc.vector.tensor_tensor(oh16[:, :, :], oh12[:, 0, :, :], oh12[:, 1, :, :], ALU.add).then_inc(v_oh, 1)
                if B_:
                    ve.wait_ge(v_rstd, b + 1)
                    nc.vector.scalar_tensor_tensor(nmr[:, :], mv[:, :, 0], -1.0, rstd[:, :], ALU.mult, ALU.mult
                                                   ).then_inc(v_nmr, 1)
                if F:
                    ve.wait_ge(a_g1, f + 1)
                    nc.vector.tensor_tensor(gq[:, :, :], g1[:, :, :], invq, ALU.mult).then_inc(v_gq, 1)
                    ve.wait_ge(s_den, f + 1)
                    after(ve, a_lnd, f)
                    nc.vector.tensor_tensor(den[:, :, :], kq_ps[:, :, :], invq, ALU.mult).then_inc(v_den, 1)
                if R:
                    ve.wait_ge(s_rk, c + 1)
                    after(ve, v_base, c)
                    nc.vector.tensor_tensor(place[:, :, :], rk_ps[:, :, :],
                                            base[:, par, :].unsqueeze(1).to_broadcast([P, T, E]), ALU.add).then_inc(v_place, 1)
                    nc.vector.tensor_tensor(base[:, 1 - par, :], base[:, par, :], tot_ps, ALU.add).then_inc(v_base, 1)
                    ve.wait_ge(a_ex, c + 1)
                    nc.vector.tensor_reduce(zs[:, :], ex[:, :, :], AX.X, ALU.add).then_inc(v_zs, 1)
                    ve.wait_ge(v_place, c + 1)
                    for k in range(2):
                        last = nc.vector.tensor_tensor(sel[:, k, :, :], oh12[:, k, :, :], place[:, :, :], ALU.mult)
                    last.then_inc(v_sel, 1)
                    ve.wait_ge(v_zs, c + 1)
                    nc.vector.reciprocal(rz[:, :], zs[:, :]).then_inc(v_rz, 1)
                    ve.wait_ge(v_sel, c + 1)
                    with nc.allow_low_precision(reason="one whole number below 2^24, the rest zeros"):
                        nc.vector.tensor_reduce(pos[:, par, :, :], sel[:, :, :, :], AX.X, ALU.add)
                    ve.wait_ge(v_rz, c + 1)
                    done(nc.vector.tensor_tensor(p2[:, :], ex2[:, :], rz[:, :], ALU.mult), v_p2, c)
                    nc.vector.scalar_tensor_tensor(ps_[:, :], p2[:, :], 1e-8, rz[:, :], ALU.add, ALU.add).then_inc(v_ps, 1)
                    low_half(c, 1)
                    ve.wait_ge(v_ps, c + 1)
                    done(nc.vector.reciprocal(rs[:, :], ps_[:, :]), v_rs, c)
                    nc.vector.tensor_tensor(rows[:, par, 0, :, D + 1], rz[:, :], rs[:, :], ALU.mult)
                    nc.vector.tensor_tensor(rows[:, par, 1, :, D + 1], p2[:, :], rs[:, :], ALU.mult).then_inc(v_row, 1)
                if F:
                    ve.wait_ge(a_tail, f + 1)
                    ve.wait_ge(v_den, f + 1)
                    done(nc.vector.scalar_tensor_tensor(lnd[:, :, :], den[:, :, :], float(D), tail[:, :, :],
                                                        ALU.add, ALU.mult), v_ndr, f)
                    done(nc.vector.scalar_tensor_tensor(lnd[:, :, :], lnd[:, :, :], -2.0, tail[:, :, :],
                                                        ALU.add, ALU.mult), v_tail, f)
                    ve.wait_ge(v_gq, f + 1)
                    after(ve, s_att, f)
                    nc.vector.scalar_tensor_tensor(mm[:, :, :], gq[:, :, :], 1.0, lnd[:, :, :],
                                                   ALU.add, ALU.mult).then_inc(v_mm, 1)
                if isinstance(f, int) and f == 0:
                    ve.wait_ge(s_const, CONST)
                    nc.vector.tensor_copy(tri16[:, :], k_sb[:, K_TRI:K_TRI + P]).then_inc(v_const, 1)
                    nc.vector.tensor_copy(base[:, 0, :], k_sb[:, K_BASE:K_BASE + E]).then_inc(v_const, 1)
                    ve.wait_ge(v_const, 2)

            def low_half(e, w):
                ve.wait_ge(s_wraw[w], 16 * (e + 1))
                if isinstance(e, int):
                    ve.wait_ge(s_whi, 16)
                    hi, lo = wsp[:, e, w, 0, :], wsp[:, e, w, 1, :]
                else:
                    hi, lo = [wsp[:, bass.ds(e, 1), w, h, :].rearrange("p o h -> p (o h)") for h in range(2)]
                nc.vector.tensor_tensor(lo, wraw[:, w, :], hi.bitcast(F32), ALU.subtract).then_inc(s_wlo, 1)

            steps(ve, step)

            def chain(ins, n=[0]):
                ins.then_inc(v_chain, 1)
                n[0] += 1
                ve.wait_ge(v_chain, n[0])

            ve.wait_ge(v_base, G)
            nc.vector.tensor_copy(pad_i[:, :], base[:, G % 2, :]).then_inc(v_tab, 1)
            chain(nc.vector.tensor_tensor(cnt[:, :], base[:, G % 2, :], k_sb[:, K_BASE:K_BASE + E], ALU.subtract))
            chain(nc.vector.tensor_tensor(over[:, :, :], cnt[:, :].unsqueeze(2).to_broadcast([P, E, NF]), thr, ALU.is_gt))
            chain(nc.vector.tensor_reduce(ntile[:, :], over[:, :, :], AX.X, ALU.add))
            chain(nc.vector.tensor_tensor_scan(cum[:, :], ones[:, 0:E], ntile[:, :], 0.0, ALU.mult, ALU.add))
            chain(nc.vector.tensor_tensor(past[:, :, :], cum[:, :].unsqueeze(1).to_broadcast([P, TILES, E]), tno, ALU.is_le))
            chain(nc.vector.tensor_tensor(pastn[:, :, :], past[:, :, :],
                                          ntile[:, :].unsqueeze(1).to_broadcast([P, TILES, E]), ALU.mult))
            chain(nc.vector.tensor_reduce(tex[:, :], past[:, :, :], AX.X, ALU.add))
            chain(nc.vector.tensor_reduce(tst[:, :], pastn[:, :, :], AX.X, ALU.add))
            chain(nc.vector.scalar_tensor_tensor(toff[:, :], tst[:, :], -float(SLOTS), tsl, ALU.mult, ALU.add))
            chain(nc.vector.scalar_tensor_tensor(trow[:, :], tex[:, :], float(REG), toff[:, :], ALU.mult, ALU.add))
            nc.vector.tensor_scalar(row_i[:, :], trow[:, :], float(E * REG), None, ALU.min).then_inc(v_tab, 1)
            nc.vector.tensor_scalar(exp_i[:, :], tex[:, :], float(E - 1), None, ALU.min).then_inc(v_tab, 1)

            def tile_step(t, n, r):
                par = r % 2
                int_t = isinstance(t, int)

                def halves(t):
                    ve.wait_ge(p_xg, t + 1)
                    after(ve, p_h, HC * t)
                    nc.vector.tensor_copy(xh[:, :], xg_ps).then_inc(v_xh, 1)
                    ve.wait_ge(v_xh, t + 1)
                    nc.vector.tensor_tensor(xl[:, :], xg_ps, xh[:, :].bitcast(F32), ALU.subtract).then_inc(v_xl, 1)

                if int_t and t == 0:
                    halves(0)
                if (not int_t or 1 <= t <= TILES):
                    ve.wait_ge(s_tile[(r - 1) % RING], 16 * ((t - 1) // RING + 1 if int_t else (n + (r > 0))))
                    if not int_t:
                        ve.wait_ge(s_ret[(r - 1) % RING], 16 * SJ * (n if r > 0 else n - 1))
                    elif t > RING:
                        ve.wait_ge(s_ret[(r - 1) % RING], 16 * SJ * ((t - 1) // RING))
                    nc.vector.tensor_copy(back[:, (r - 1) % RING, :, :].bitcast(I32), xg[:, (r - 1) % RING, :, D:D + 2].bitcast(I32)
                                          ).then_inc(v_back, 1)
                if within(t):
                    for m in range(HC):
                        ve.wait_ge(a_h, HC * t + m + 1)
                        after(ve, p_y, t - 1)
                        nc.vector.tensor_copy(hh[:, par, m, :], h_sb[:, m, :]).then_inc(v_hh, 1)
                        ve.wait_ge(v_hh, HC * t + m + 1)
                        nc.vector.tensor_tensor(hl[:, par, m, :], h_sb[:, m, :], hh[:, par, m, :].bitcast(F32),
                                                ALU.subtract).then_inc(v_hl, 1)
                        if m == 1 and (not int_t or t + 1 < TILES):
                            halves(t + 1)

            tiles(ve, tile_step)

            for c in range(G + 1):
                if c < G:
                    q = c % 2

                    def link(ins, s):
                        ins.then_inc(s, 1)
                        ve.wait_ge(s, c + 1)
                    xs = x1_all[:, T * c:T * (c + 1), :].rearrange("p t d -> p (t d)")
                    ve.wait_ge(s_y1[q], 16 * (c // 2 + 1))
                    ve.wait_ge(s_y2[q], 16 * (c // 2 + 1))
                    link(nc.vector.tensor_tensor(x_sb[:, q, :], x_sb[:, q, :], xT_sb[:, q, :], ALU.add), f_z1)
                    link(nc.vector.tensor_tensor(xs, xs, x_sb[:, q, :], ALU.add), f_z)
                    for t in range(T):
                        last = nc.vector.bn_stats(st6[:, t, :], x1_all[:, T * c + t, :])
                    link(last, f_st)
                    after(ve, f_nmr, c - 1)
                    for t in range(T):
                        last = nc.vector.bn_aggr(mv2[:, q, t, :], st6[:, t, :])
                    link(last, f_mv)
                if c >= 1:
                    ve.wait_ge(g_rstd, c)
                    after(ve, g_out, c - 1)
                    for ins, s_ in ((lambda: nc.vector.scalar_tensor_tensor(nwt[:, :], var[:, :], -0.5, rstd0[:, :], ALU.mult, ALU.mult), f_nwt),
                                    (lambda: nc.vector.tensor_tensor(nwt2[:, :], nwt[:, :], rstd0[:, :], ALU.mult), f_nwt2),
                                    (lambda: nc.vector.scalar_tensor_tensor(rstd[:, :], nwt2[:, :], 1.5, rstd0[:, :], ALU.add, ALU.mult), f_rstd)):
                        ins().then_inc(s_, 1)
                        ve.wait_ge(s_, c)
                    nc.vector.scalar_tensor_tensor(nmr[:, :], mv2[:, 1 - c % 2, :, 0], -1.0, rstd[:, :],
                                                   ALU.mult, ALU.mult).then_inc(f_nmr, 1)
                if c < G:
                    nc.vector.tensor_scalar(var[:, :], mv2[:, q, :, 1], EPS_LN, None, ALU.add).then_inc(f_var, 1)

        @block.gpsimd
        def _(pool):
            def scatter(c, par):
                pool.wait_ge(a_rows, c + 1)
                pool.wait_ge(v_row, c + 1)
                pool.sem_inc(g_turn, 1)
                for k in range(2):
                    for t in range(T):
                        nc.gpsimd.indirect_dma_start(
                            regions, bass.IndirectOffsetOnAxis(ap=pos[:, par, k, t:t + 1], axis=0),
                            rows[:, par, k, t, :], None).then_inc(s_scat[par], 16)
                    if k == 0 and not (isinstance(c, int) and c == 0):
                        pool.wait_ge(s_scat[1 - par], loaded(c - 1, 1 - par) * 2 * T)
                        pool.sem_inc(g_free, 1)

            pool.sem_inc(g_free, 2)
            pool.wait_ge(s_x[1], 16)
            pool.dma_start(wsp[:, :, :, 0, :].rearrange("p e w h -> p (e w) h"),
                           wts.rearrange("p e w h -> p (e w) h")).then_inc(s_whi, 16)
            scatter(0, 0)
            with pool.Fori(1, G // 2) as i:
                scatter(2 * i - 1, 1)
                scatter(2 * i, 0)
            scatter(G - 1, 1)

            last_row = pool.to_reg(2 * TOK - 1)

            def tile_step(t, n, r):
                if not isinstance(t, int) or 0 <= t - 2 < TILES:
                    pool.wait_ge(a_yo, t - 1)
                    pool.sem_inc(g_turn, 1)
                    for j in range(SJ):
                        nc.gpsimd.indirect_dma_start(
                            returned, bass.IndirectOffsetOnAxis(ap=back[:, (r - 2) % RING, j, 0:1].bitcast(I32), axis=0),
                            yo[:, r % 2, j, :], None, bounds_check=last_row, oob_is_err=False
                        ).then_inc(s_ret[(r - 2) % RING], 16)

            tiles(pool, tile_step)
            for r in range(RING):
                pool.wait_ge(s_ret[r], 16 * SJ * len(range(r, TILES, RING)))


def kernel(L0_attn_x, L0_attn_Wq, L0_attn_bq, L0_attn_Wk, L0_attn_bk, L0_attn_Wv, L0_attn_bv, L0_attn_gamma,
           L0_ffn_router_w, L0_ffn_w1, L0_ffn_b1, L0_ffn_w2, L0_ffn_b2):
    import concourse.bacc as _bacc
    from concourse.bass_utils import run_bass_kernel_spmd as _run

    x = np.ascontiguousarray(L0_attn_x).reshape(TOK, D)
    w1T = np.transpose(L0_ffn_w1, (0, 2, 1))
    w2T = np.transpose(np.reshape(L0_ffn_w2, (E, D, HC, P)), (0, 3, 2, 1)).reshape(E, P, H)
    b1c = np.transpose(np.reshape(L0_ffn_b1, (E, HC, P)), (2, 0, 1))
    b2c = np.transpose(L0_ffn_b2, (1, 0))[:, :, None]
    consts = np.zeros((P, K_COLS), np.float32)
    consts[:, K_ID:K_ID + P] = np.eye(P)
    consts[:, K_TRI:K_TRI + P] = np.triu(np.ones((P, P)), 1)
    consts[:, K_REV:K_REV + T * E] = np.tile(E - np.arange(E), T)
    consts[:, K_BASE:K_BASE + E] = REG * np.arange(E)
    consts[:, K_THR:K_T] = np.tile(SLOTS * np.arange(NF), E)
    consts[:, K_T:K_TS] = np.repeat(np.arange(TILES), E)
    consts[:, K_TS:K_COLS] = SLOTS * np.arange(TILES)
    returns = (np.arange(P)[:, None, None, None] + GC * np.arange(G)[None, :, None, None]
               + TOK * np.arange(2)[None, None, :, None] + P * np.arange(T)[None, None, None, :]).astype(np.int32)
    arrays = {
        "x": x,
        "xT": x.T,
        "cols": np.concatenate([np.transpose(L0_attn_Wq), np.transpose(L0_attn_Wk), np.transpose(L0_attn_Wv),
                                np.transpose(L0_ffn_router_w), np.reshape(L0_attn_bv, (D, 1))], axis=1),
        "vecs": np.concatenate([L0_attn_bq, L0_attn_bk, L0_attn_gamma]),
        "wts": np.stack([np.transpose(w1T, (1, 0, 2)), np.transpose(w2T, (1, 0, 2))], axis=2),
        "bcols": np.concatenate([b1c, b2c], axis=2),
        "consts": consts,
        "returns": returns,
    }
    arrays = {"in_" + k: np.ascontiguousarray(v) for k, v in arrays.items()}
    nc = _bacc.Bacc("TRN2", target_bir_lowering=False, num_devices=1)
    args = [nc.dram_tensor(k, v.shape, mybir.dt.from_np(v.dtype), kind="ExternalInput").ap() for k, v in arrays.items()]
    args.append(nc.dram_tensor("out_0", (TOK, D), F32, kind="ExternalOutput").ap())
    args.append(nc.dram_tensor("regions", ((E + 1) * REG, ROW), F32, kind="Internal").ap())
    args.append(nc.dram_tensor("returned", (2 * TOK, D), F32, kind="Internal").ap())
    moe_layer(nc, *args)
    r = _run(nc, [arrays], core_ids=[0])
    return r.results[0]["out_0"].reshape(B, C, D)
```

```python
from contextlib import ExitStack

import numpy as np

import concourse.bass as bass
from concourse import mybir

P = 128
B, C, D = 16, 256, 128
TOK = B * C
E = 8
H = 4 * D
HC = H // P
NT = TOK // P
GB = 2
T = GB * C // P
G = B // GB
GC = T * P
SLOTS = 512
SJ = SLOTS // P
TILES = (2 * TOK - E) // SLOTS + E
NF = -(-TOK // SLOTS)
REG = TOK + SLOTS
ROW = D + 2
SKIP = 1 << 20
EPS_K = 1e-6
EPS_LN = 1e-5
NEG = -1e30
ACT_GELU = "gelu_apprx_tanh_and_others"
ACT_LN_EXP = "natural_log_exp_and_others"

F32 = mybir.dt.float32
F32R = mybir.dt.float32r
BF16 = mybir.dt.bfloat16
I32 = mybir.dt.int32
ALU = mybir.AluOpType
ACT = mybir.ActivationFunctionType
AX = mybir.AxisListType

K_ID, K_TRI, K_REV, K_BASE = 0, P, 2 * P, 2 * P + T * E
K_THR = K_BASE + E
K_T = K_THR + E * NF
K_TS = K_T + TILES * E
K_COLS = K_TS + TILES
RING = 4
XV = 2
BT = 2 * T
YRING = 4


def moe_layer(nc, x, xT, cols, vecs, wts, bcols, consts, returns, out,
              regions, returned):
    with ExitStack() as ctx:
        def sb(name, shape, dt=F32):
            return ctx.enter_context(nc.sbuf_tensor(name, shape, dt))

        def psum(name, shape):
            return ctx.enter_context(nc.psum_tensor(name, shape, F32))

        def sem(name):
            return ctx.enter_context(nc.semaphore(name))

        bank = psum("bank", [P, 8, 512])
        qk_ps = bank[:, 0:2, :]
        vT_ps = bank[:, 2, :]
        kq_ps = bank[:, 3, 0:GB * D].rearrange("p (b n) -> p b n", b=GB)
        qss_ps = bank[:, 4, 0:GB * D].rearrange("p (b n) -> p b n", b=GB)
        kss_ps = bank[:, 4, GB * D:GB * D + GB]
        ss_ps = bank[:, 4, 0:GB * D + GB]
        att_ps = bank[:, 5, :]
        x1T_ps = bank[:, 6, :]
        lg_ps = bank[:, 7, 0:T * E].rearrange("p (t e) -> p t e", t=T)
        rk_ps = bank[:, 7, 64:64 + T * E].rearrange("p (t e) -> p t e", t=T)
        tot_ps = bank[:, 7, 128:128 + E]

        k_sb = sb("k_sb", [P, K_COLS])
        ident = k_sb[:, K_ID:K_ID + P]
        rev = k_sb[:, K_REV:K_REV + T * E].rearrange("p (t e) -> p t e", t=T)
        ret_sb = sb("ret_sb", [P, G, 2, T], I32)
        cols_sb = sb("cols_sb", [P, 3 * D + E + 1])
        wqk_sb, wv_sb = cols_sb[:, 0:2 * D], cols_sb[:, 2 * D:3 * D]
        rw_sb, bv_sb = cols_sb[:, 3 * D:3 * D + E], cols_sb[:, 3 * D + E:3 * D + E + 1]
        vecs_sb = sb("vecs_sb", [P, 2 * D + 1])
        bqk_sb, gam_sb = vecs_sb[:, 0:2 * D], vecs_sb[:, 2 * D:2 * D + 1]
        gam2 = sb("gam2", [P, 1])
        bcol_sb = sb("bcol_sb", [P, E, HC + 1])
        ones = sb("ones", [P, P])
        epsm = sb("epsm", [P, P])
        width = sb("width", [P, 1])
        tri16 = sb("tri16", [P, P], BF16)
        ones16 = sb("ones16", [P, P], BF16)

        x_sb = sb("x_sb", [P, 2, T * D])
        xT_sb = sb("xT_sb", [P, 2, GC])
        work = sb("work", [P, 2, T * 2 * D])
        qk = work[:, 0, :].rearrange("p (t n) -> p t n", t=T)
        qk2 = work[:, 1, :].rearrange("p (t n) -> p t n", t=T)
        x1s = sb("x1s", [P, T, D])
        vT = sb("vT", [P, GC])
        lnss = sb("lnss", [P, GB * D + GB])
        inv = sb("inv", [P, GB * D + GB])
        invq = inv[:, 0:GB * D].rearrange("p (b n) -> p b n", b=GB)
        invk = inv[:, GB * D:GB * D + GB]
        g1 = sb("g1", [P, GB, D])
        gq = sb("gq", [P, GB, D])
        den = sb("den", [P, GB, D])
        lnd = sb("lnd", [P, GB, D])
        ndr = lnd[:, :, :]
        tail = sb("tail", [P, GB, D])
        ntail = sb("ntail", [P, GB, D])
        mm = sb("mm", [P, GB, D])
        z = sb("z", [P, T, D])
        st6 = sb("st6", [P, T, 6])
        mv = sb("mv", [P, T, 2])
        var = sb("var", [P, T])
        lnv = sb("lnv", [P, T])
        rstd0 = sb("rstd0", [P, T])
        nwt = sb("nwt", [P, T])
        nwt2 = sb("nwt2", [P, T])
        rstd = sb("rstd", [P, T])
        nmr = sb("nmr", [P, T])
        rows = sb("rows", [P, 2, 2, T, ROW])
        rows_i = rows[:, :, :, :, :].bitcast(I32)
        x1T = sb("x1T", [P, GC])
        x1_all = sb("x1_all", [P, NT, D])

        m1 = sb("m1", [P, T])
        dl = sb("dl", [P, T, E])
        key1 = sb("key1", [P, T, E])
        km1 = sb("km1", [P, T])
        oh12 = sb("oh12", [P, 2, T, E])
        dl2 = sb("dl2", [P, T, E])
        m2 = sb("m2", [P, T])
        eq2 = sb("eq2", [P, T, E])
        key2 = sb("key2", [P, T, E])
        km2 = sb("km2", [P, T])
        oh16 = sb("oh16", [P, T, E], BF16)
        base = sb("base", [P, 2, E])
        place = sb("place", [P, T, E])
        sel = sb("sel", [P, 2, T, E])
        sel_ke, oh12_ke = [a[:, :, :, :].rearrange("p k t e -> p k (t e)") for a in (sel, oh12)]
        place_e = place[:, :, :].rearrange("p t e -> p (t e)")
        pos = sb("pos", [P, 2, 2, T], I32)
        ex = sb("ex", [P, T, E])
        ex2 = sb("ex2", [P, T])
        zs = sb("zs", [P, T])
        p12 = sb("p12", [P, 2, T])
        rz, p2 = p12[:, 0, :], p12[:, 1, :]
        ps_ = sb("ps_", [P, T])
        rs = sb("rs", [P, T])

        thr = k_sb[:, K_THR:K_THR + E * NF].rearrange("p (e n) -> p e n", e=E)
        tno = k_sb[:, K_T:K_T + TILES * E].rearrange("p (t e) -> p t e", t=TILES)
        tsl = k_sb[:, K_TS:K_TS + TILES]
        cnt = sb("cnt", [P, E])
        over = sb("over", [P, E, NF])
        ntile = sb("ntile", [P, E])
        cum = sb("cum", [P, E])
        past = sb("past", [P, TILES, E])
        pastn = sb("pastn", [P, TILES, E])
        tex = sb("tex", [P, TILES])
        tst = sb("tst", [P, TILES])
        toff = sb("toff", [P, TILES])
        trow = sb("trow", [P, TILES])
        row_i = sb("row_i", [P, TILES], I32)
        exp_i = sb("exp_i", [P, TILES], I32)
        pad_i = sb("pad_i", [P, E], I32)

        h_ps = bank[:, 0:HC, 0:SLOTS]
        xg_ps = bank[:, 4, 0:SLOTS]
        y_ps = bank[:, 5, 0:SLOTS]
        yt_ps = bank[:, 6, 0:SLOTS]
        pad_sb = sb("pad_sb", [P, SJ, ROW])
        wraw = sb("wraw", [P, 2, H])
        wsp = sb("wsp", [P, E, 2, 2, H], F32R)
        w1st = sb("w1st", [P, 2, 2, H], F32R)
        w2st = sb("w2st", [P, 2, 2, H], F32R)
        bst = sb("bst", [P, RING, HC + 1])
        xg = sb("xg", [P, RING, SJ, ROW])
        xh = sb("xh", [P, SLOTS], F32R)
        xl = sb("xl", [P, SLOTS], F32R)
        h_sb = work[:, :, :].rearrange("p a (m s) -> p (a m) s", m=HC // 2)[:, :, 0:SLOTS]
        hh = sb("hh", [P, 2, HC, SLOTS], F32R)
        hl = sb("hl", [P, 2, HC, SLOTS], F32R)
        y_sb = sb("y_sb", [P, SLOTS])
        yo = sb("yo", [P, 2, SJ, D])
        back = sb("back", [P, RING, SJ, 2])

        y1 = [x_sb[:, 0, :], x_sb[:, 1, :], work[:, 0, 0:T * D], work[:, 1, 0:T * D]]
        y2 = [xT_sb[:, 0, :], xT_sb[:, 1, :], work[:, 0, T * D:2 * T * D], work[:, 1, T * D:2 * T * D]]
        fmv = sb("fmv", [P, 2, BT, 2])
        fvar, flnv, frstd0, fnwt, fnwt2, frstd, fnmr = [sb("f" + n, [P, BT]) for n in (
            "var", "lnv", "rstd0", "nwt", "nwt2", "rstd", "nmr")]

        raw_xg = xg[:, :, :, :].rearrange("p r j c -> p (r j c)")[:, 0:4 * H].rearrange("p (n h) -> p n h", h=H)
        raw_yo = yo[:, :, :, :].rearrange("p r j d -> p (r j d)").rearrange("p (n h) -> p n h", h=H)
        RAW_XG, RAW_YO, RAW_END = E, E + 4, E + 6

        s_cols, s_vecs, s_const, s_set = [sem(n) for n in ("s_cols", "s_vecs", "s_const", "s_set")]
        s_x = [sem("s_x0"), sem("s_x1")]
        s_xT = [sem("s_xT0"), sem("s_xT1")]
        (s_qk, s_vT, s_kq, s_stat, s_den, s_att, s_xt, s_lg, s_rk) = [sem("pe_" + n) for n in (
            "qk", "vT", "kq", "stat", "den", "att", "xt", "lg", "rk")]
        (a_lnv, a_rstd, a_x1, a_vT, a_sq, a_lnss, a_inv, a_x1T, a_g1, a_rows, a_ex, a_lnd, a_tail) = [
            sem("act_" + n) for n in ("lnv", "rstd", "x1", "vT", "sq", "lnss", "inv", "x1T", "g1", "rows", "ex",
                                      "lnd", "tail")]
        (v_z, v_st, v_mv, v_var, v_nwt, v_nwt2, v_rstd, v_nmr, v_x1, v_qk, v_den, v_gq, v_ndr, v_tail, v_mm, v_m1,
         v_dl, v_key1, v_km1, v_oh1, v_dl2, v_m2, v_eq2, v_key2, v_km2, v_oh2, v_oh, v_place,
         v_base, v_sel, v_zs, v_rz, v_p2, v_ps, v_rs, v_row) = [sem("dve_" + n) for n in (
            "z", "st", "mv", "var", "nwt", "nwt2", "rstd", "nmr", "x1", "qk", "den", "gq", "ndr", "tail", "mm", "m1",
            "dl", "key1", "km1", "oh1", "dl2", "m2", "eq2", "key2", "km2", "oh2", "oh", "place",
            "base", "sel", "zs", "rz", "p2", "ps", "rs", "row")]
        s_scat = [sem("s_scat0"), sem("s_scat1")]
        g_free = sem("pool_rows_free")
        s_keep = sem("s_keep")
        SCAT = 16 * 2 * T
        s_done = [sem("s_done0"), sem("s_done1")]
        s_pad0 = sem("s_pad0")
        s_wraw = [sem("s_wraw0"), sem("s_wraw1")]
        s_raw = sem("s_raw")
        s_whi, s_wlo = sem("s_whi"), sem("s_wlo")
        v_tab = sem("dve_table")
        v_const = sem("dve_const")
        g_turn = sem("pool_turn")
        v_chain = sem("dve_chain")
        s_pads = sem("s_pads")
        s_tile = [sem(f"s_tile{r}") for r in range(RING)]
        s_bst = [sem(f"s_bst{r}") for r in range(RING)]
        s_w1 = [sem("s_w1st0"), sem("s_w1st1")]
        s_w2 = [sem("s_w2st0"), sem("s_w2st1")]
        p_xg, p_h, p_y, p_yt = [sem("pe_" + n) for n in ("xg", "h", "y", "ytr")]
        a_h, a_y, a_yo = [sem("act_" + n) for n in ("h", "y", "yo")]
        v_pad, v_xh, v_xl, v_hh, v_hl, v_back = [sem("dve_" + n) for n in ("pad", "xh", "xl", "hh", "hl", "back")]
        s_ret = [sem(f"s_ret{r}") for r in range(RING)]
        s_y = [sem(f"s_y{r}") for r in range(YRING)]
        g_z1 = sem("pool_z1")
        SET, CONST = 5, 16 * 3
        (f_z, f_st, f_mv, f_var, f_nwt, f_nwt2, f_rstd, f_nmr, f_out) = [sem("fin_" + n) for n in (
            "z", "st", "mv", "var", "nwt", "nwt2", "rstd", "nmr", "out")]
        g_lnv, g_rstd, g_out = [sem("fina_" + n) for n in ("lnv", "rstd", "out")]

        block = ctx.enter_context(nc.Block())

        def steps(eng, step):
            step(0, None, None, 0)
            step(1, 0, None, 1)
            step(2, 1, 0, 0)
            with eng.Fori(1, G // 2 - 1) as i:
                step(2 * i + 1, 2 * i, 2 * i - 1, 1)
                step(2 * i + 2, 2 * i + 1, 2 * i, 0)
            step(G - 1, G - 2, G - 3, 1)
            step(None, G - 1, G - 2, 0)
            step(None, None, G - 1, 1)

        def more(f):
            return f is not None and (not isinstance(f, int) or f + 1 < G)

        def loaded(g, par):
            return 16 * (g // 2 + 1) if isinstance(g, int) else 8 * (g + 2 - par)

        def after(eng, s, n):
            if not isinstance(n, int) or n > 0:
                eng.wait_ge(s, n)

        def tiles(eng, step):
            last = (TILES - 3) // RING
            for t in range(RING + 1):
                step(t, t // RING, t % RING)
            with eng.Fori(1, last) as i:
                for k in range(1, RING + 1):
                    step(RING * i + k, i + k // RING, k % RING)
            for t in range(RING * last + 1, TILES + 2):
                step(t, t // RING, t % RING)

        def vector_share(k):
            return T if k == G // 2 - 1 else 0

        def within(t):
            return not isinstance(t, int) or 0 <= t < TILES

        @block.sync
        def _(sp):
            x_groups = x.rearrange("(g t p) d -> g p t d", t=T, p=P)
            xT_groups = xT.rearrange("d (g n) -> g d n", n=GC)

            def load_xT(g, par):
                src = xT_groups[g] if isinstance(g, int) else xT_groups[bass.ds(g, 1)].rearrange("o d n -> d (o n)")
                sp.dma_start(xT_sb[:, par, :], src).then_inc(s_xT[par], 16)

            def load_x(g, par):
                src = x_groups[g] if isinstance(g, int) else x_groups[bass.ds(g, 1)].rearrange("o p t d -> p (o t) d")
                sp.dma_start(x_sb[:, par, :].rearrange("p (t d) -> p t d", t=T), src).then_inc(s_x[par], 16)

            wts_n = wts.rearrange("p e w h -> p (e w) h")

            def load_raw(n, buf):
                src = wts_n[:, n, :] if isinstance(n, int) else wts_n[:, bass.ds(n, 1), :].rearrange("p o h -> p (o h)")
                sp.dma_start(wraw[:, buf, :], src).then_inc(s_wraw[buf], 16)

            def load_step(s, par):
                if not isinstance(s, int) or s + 2 < G:
                    sp.wait_ge(s_vT, s + 1)
                    load_xT(s + 2, par)
                if not isinstance(s, int) or s + 1 < G:
                    sp.wait_ge(v_z, s)
                    load_x(s + 1, 1 - par)
                after(sp, s_wlo, s - 2)
                load_raw(s - 1, 1 - par)
                sp.wait_ge(a_x1, s)
                sp.wait_ge(v_x1, s)
                dst = x1_all[:, T * (s - 1):T * s, :] if isinstance(s, int) else x1_all[:, bass.ds(T * (s - 1), T), :]
                sp.dma_start(dst, x1s[:, :, :]).then_inc(s_keep, 16)

            load_xT(0, 0)
            sp.dma_start(cols_sb[:, :], cols).then_inc(s_cols, 16)
            sp.dma_start(vecs_sb[:, :], vecs.partition_broadcast(P)).then_inc(s_vecs, 16)
            load_xT(1, 1)
            load_x(0, 0)
            load_x(1, 1)
            for dst, src in ((k_sb[:, :], consts), (ret_sb[:, :, :, :], returns), (bcol_sb[:, :, :], bcols)):
                sp.dma_start(dst, src).then_inc(s_const, 16)
            sp.wait_ge(s_vT, 1)
            load_xT(2, 0)
            load_step(1, 1)
            sp.dma_start(raw_xg, wts_n[:, RAW_XG:RAW_YO, :]).then_inc(s_raw, 16)
            sp.dma_start(raw_yo, wts_n[:, RAW_YO:RAW_END, :]).then_inc(s_raw, 16)
            sp.wait_ge(v_pad, 2)
            sp.dma_start(regions[E * REG:E * REG + SLOTS, :].rearrange("(p j) c -> p j c", j=SJ),
                         pad_sb[:, :, :]).then_inc(s_pad0, 16)
            with sp.Fori(1, G // 2 - 1) as i:
                load_step(2 * i, 0)
                load_step(2 * i + 1, 1)
            for s in range(G - 2, G + 1):
                load_step(s, s % 2)
            for n in range(RAW_END, 2 * E):
                sp.wait_ge(s_wlo, n - RAW_END + E - 1)
                load_raw(n, n % 2)
            sp.wait_ge(v_tab, 1)
            for e in range(E):
                row = sp.value_load(pad_i[0:1, e:e + 1], min_val=e * REG, max_val=e * REG + TOK)
                sp.dma_start(regions[bass.ds(row, SLOTS), :].rearrange("(p j) c -> p j c", j=SJ),
                             pad_sb[:, :, :]).then_inc(s_pads, 16)
            def load_tile(t, n, r):
                after(sp, v_back, t - RING + 1)
                row = sp.value_load(row_i[0:1, t:t + 1] if isinstance(t, int) else row_i[0:1, bass.ds(t, 1)],
                                    min_val=0, max_val=E * REG)
                sp.dma_start(xg[:, r, :, :], regions[bass.ds(row, SLOTS), :].rearrange("(p j) c -> p j c", j=SJ)
                             ).then_inc(s_tile[r], 16)

            def expert(t):
                return sp.value_load(exp_i[0:1, t:t + 1] if isinstance(t, int) else exp_i[0:1, bass.ds(t, 1)],
                                     min_val=0, max_val=E - 1)

            def load_first(t, e, r):
                after(sp, p_h, HC * (t - 1))
                sp.dma_start(w1st[:, r % 2, :, :].bitcast(F32),
                             wsp[:, bass.ds(e, 1), 0, :, :].bitcast(F32).rearrange("p o a h -> p (o a) h")
                             ).then_inc(s_w1[r % 2], 16)
                after(sp, a_y, t - RING + 1)
                sp.dma_start(bst[:, r, :], bcol_sb[:, bass.ds(e, 1), :].rearrange("p o a -> p (o a)")
                             ).then_inc(s_bst[r], 16)

            def load_step(t, n, r):
                if within(t):
                    e = expert(t)
                if within(t) and (not isinstance(t, int) or t + 2 < TILES):
                    load_tile(t + 2, None, (r + 2) % RING)
                if within(t) and (not isinstance(t, int) or t + 1 < TILES):
                    load_first(t + 1, expert(t + 1), (r + 1) % RING)
                if within(t):
                    after(sp, p_y, t - 1)
                    sp.dma_start(w2st[:, r % 2, :, :].bitcast(F32),
                                 wsp[:, bass.ds(e, 1), 1, :, :].bitcast(F32).rearrange("p o a h -> p (o a) h")
                                 ).then_inc(s_w2[r % 2], 16)

            sp.wait_ge(s_wlo, 2 * E)
            sp.wait_ge(v_tab, 3)
            load_first(0, expert(0), 0)
            for q in range(2):
                sp.wait_ge(s_scat[q], SCAT * (G // 2))
            sp.wait_ge(s_keep, 16 * G)
            sp.wait_ge(s_pads, 16 * E)
            sp.wait_ge(s_pad0, 16)
            load_tile(0, 0, 0)
            load_tile(1, 0, 1)
            tiles(sp, load_step)

            for r in range(RING):
                sp.wait_ge(s_ret[r], 16 * SJ * len(range(r, TILES, RING)))
            ret = returned.rearrange("(k g t p) d -> k g p t d", k=2, t=T, p=P)
            outg = out.rearrange("(g t p) d -> g p t d", t=T, p=P)
            for c in range(G):
                after(sp, f_z, c - YRING + 1)
                sp.dma_start(y1[c % YRING].rearrange("p (t d) -> p t d", t=T), ret[0, c]).then_inc(s_y[c % YRING], 16)
                sp.dma_start(y2[c % YRING].rearrange("p (t d) -> p t d", t=T), ret[1, c]).then_inc(s_y[c % YRING], 16)
            for c in range(G):
                if c < G - 1:
                    sp.wait_ge(g_out, c + 1)
                else:
                    sp.wait_ge(f_out, 1)
                sp.dma_start(outg[c], x1_all[:, T * c:T * (c + 1), :]).then_inc(s_done[c % 2], 16)
            for q in range(2):
                sp.wait_ge(s_done[q], 16 * (G // 2))

        @block.tensor
        def _(pe):
            def project_qk(g, par, b):
                for t in range(b * C // P, (b + 1) * C // P):
                    last = nc.tensor.matmul(qk_ps[:, b, t % 2 * 2 * D:(t % 2 + 1) * 2 * D],
                                            xT_sb[:, par, t * P:(t + 1) * P], wqk_sb, start=True, stop=True)
                last.then_inc(s_qk, 1)

            def column_sums(f, b):
                pe.wait_ge(a_sq, GB * f + b + 1)
                after(pe, a_lnss, f)
                tiles_b = range(b * C // P, (b + 1) * C // P)
                for t in tiles_b:
                    nc.tensor.matmul(qss_ps[:, b, :], ones[:, :], qk2[:, t, 0:D],
                                     start=t == tiles_b[0], stop=t == tiles_b[-1])
                for t in tiles_b:
                    last = nc.tensor.matmul(kss_ps[:, b:b + 1], qk2[:, t, D:2 * D], ones[:, 0:1],
                                            start=t == tiles_b[0], stop=t == tiles_b[-1])
                last.then_inc(s_stat, 1)

            def project_v(g, par):
                after(pe, a_vT, g)
                nc.tensor.matmul(vT_ps, wv_sb, xT_sb[:, par, :], start=True, stop=True).then_inc(s_vT, 1)

            def step(f, b, c, par):
                if c is not None:
                    pe.wait_ge(a_x1, c + 1)
                    pe.wait_ge(v_x1, c + 1)
                    after(pe, a_x1T, c)
                    for t in range(T):
                        last = nc.tensor.transpose(x1T_ps[:, t * P:(t + 1) * P], x1s[:, t, :], ident)
                    last.then_inc(s_xt, 1)
                if f is not None:
                    column_sums(f, 0)
                if b is not None:
                    pe.wait_ge(v_mm, b + 1)
                    after(pe, v_z, b)
                    for t in range(T):
                        last = nc.tensor.matmul(att_ps[:, t * D:(t + 1) * D], vT[:, t * P:(t + 1) * P],
                                                mm[:, t * P // C, :], start=True, stop=True)
                    last.then_inc(s_att, 1)
                if c is not None:
                    pe.wait_ge(a_x1T, c + 1)
                    after(pe, v_base, c)
                    for t in range(T):
                        last = nc.tensor.matmul(lg_ps[:, t, :], x1T[:, t * P:(t + 1) * P], rw_sb, start=True, stop=True)
                    last.then_inc(s_lg, 1)
                if f is not None:
                    column_sums(f, 1)
                    pe.wait_ge(v_qk, GB * f + GB)
                    after(pe, v_den, f)
                    for t in range(T):
                        last = nc.tensor.matmul(kq_ps[:, t * P // C, :], qk[:, t, D:2 * D], qk[:, t, 0:D],
                                                start=t * P % C == 0, stop=(t + 1) * P % C == 0)
                    last.then_inc(s_kq, 1)
                if more(f):
                    pe.wait_ge(s_xT[1 - par], loaded(f + 1, 1 - par))
                    project_qk(f + 1, 1 - par, 0)
                if f is not None:
                    pe.wait_ge(a_g1, f + 1)
                    for q in range(GB):
                        for t in range(q * C // P, (q + 1) * C // P):
                            nc.tensor.matmul(kq_ps[:, q, :], epsm[:, :], qk[:, t, 0:D],
                                             start=t * P % C == 0, stop=False)
                        last = nc.tensor.matmul(kq_ps[:, q, :], ones[:, :], g1[:, q, :], start=False, stop=True)
                    last.then_inc(s_den, 1)
                if c is not None:
                    pe.wait_ge(v_oh, c + 1)
                    if isinstance(c, int) and c == 0:
                        pe.wait_ge(v_const, 2)
                    nc.tensor.matmul(rk_ps[:, :, :], tri16[:, :], oh16[:, :, :], start=True, stop=True)
                    for t in range(T - 1):
                        for u in range(t + 1, T):
                            nc.tensor.matmul(rk_ps[:, u, :], ones16[:, :], oh16[:, t, :], start=False,
                                             stop=True, skip_group_check=True)
                    for t in range(T):
                        last = nc.tensor.matmul(tot_ps, ones16[:, :], oh16[:, t, :], start=t == 0, stop=t == T - 1,
                                                skip_group_check=True)
                    last.then_inc(s_rk, 1)
                if more(f):
                    project_qk(f + 1, 1 - par, 1)
                    project_v(f + 1, 1 - par)

            pe.wait_ge(s_xT[0], 16)
            pe.wait_ge(s_cols, 16)
            for b in range(GB):
                project_qk(0, 0, b)
            project_v(0, 0)
            pe.wait_ge(s_set, SET)
            pe.wait_ge(s_const, CONST)
            steps(pe, step)

            def tile_step(t, n, r):
                par = r % 2
                int_t = isinstance(t, int)

                def transposed(t, n, r):
                    pe.wait_ge(s_tile[r], 16 * (n + 1))
                    after(pe, v_xl, t)
                    for j in range(SJ):
                        last = nc.tensor.transpose(xg_ps[:, j * P:(j + 1) * P], xg[:, r, j, 0:D], ident)
                    last.then_inc(p_xg, 1)

                if int_t and t == 0:
                    pe.wait_ge(v_base, G)
                    pe.wait_ge(a_x1T, G)
                    pe.wait_ge(v_z, G)
                    pe.wait_ge(v_mm, G)
                    pe.wait_ge(s_scat[1], SCAT * (G // 2))
                    for _ in range(8):
                        nc.tensor.matmul(y_ps[:, 0:P], ones[:, :], ones[:, :], start=True, stop=True)
                    transposed(0, 0, 0)
                if within(t):
                    pe.wait_ge(s_w1[par], 16 * (t // 2 + 1) if int_t else 8 * (t - par) + 16)
                    pe.wait_ge(v_xl, t + 1)
                    for m in range(HC):
                        cols = slice(m * P, (m + 1) * P)
                        after(pe, a_h, HC * (t - 1) + m + 1)
                        nc.tensor.matmul(h_ps[:, m, :], w1st[:, par, 0, cols], xh[:, :], start=True, stop=False)
                        nc.tensor.matmul(h_ps[:, m, :], w1st[:, par, 0, cols], xl[:, :], start=False, stop=False)
                        nc.tensor.matmul(h_ps[:, m, :], w1st[:, par, 1, cols], xh[:, :], start=False, stop=True
                                         ).then_inc(p_h, 1)
                if within(t) and (not int_t or t + 1 < TILES):
                    transposed(t + 1, n + (r == RING - 1), (r + 1) % RING)
                if (not int_t or t >= 2) and (not int_t or t - 2 < TILES):
                    pe.wait_ge(a_y, t - 1)
                    after(pe, a_yo, t - 2)
                    for j in range(SJ):
                        last = nc.tensor.transpose(yt_ps[:, j * P:(j + 1) * P], y_sb[:, j * P:(j + 1) * P], ident)
                    last.then_inc(p_yt, 1)
                if (not int_t or 1 <= t <= TILES):
                    pe.wait_ge(s_w2[1 - par], 16 * ((t - 1) // 2 + 1) if int_t else 8 * (t + par))
                    after(pe, a_y, t - 1)
                    for m in range(HC):
                        cols = slice(m * P, (m + 1) * P)
                        pe.wait_ge(v_hl, HC * (t - 1) + m + 1)
                        nc.tensor.matmul(y_ps, w2st[:, 1 - par, 0, cols], hh[:, 1 - par, m, :], start=m == 0, stop=False)
                        nc.tensor.matmul(y_ps, w2st[:, 1 - par, 0, cols], hl[:, 1 - par, m, :], start=False, stop=False)
                        last = nc.tensor.matmul(y_ps, w2st[:, 1 - par, 1, cols], hh[:, 1 - par, m, :], start=False,
                                                stop=m == HC - 1)
                    last.then_inc(p_y, 1)

            tiles(pe, tile_step)

        @block.scalar
        def _(act):
            def square(g, b):
                act.wait_ge(v_qk, GB * g + b + 1)
                after(act, s_stat, GB * (g - 1) + b + 1)
                nc.scalar.activation(qk2[:, 2 * b:2 * b + 2, :], qk[:, 2 * b:2 * b + 2, :], ACT.Square).then_inc(a_sq, 1)

            def step(f, b, c, par):
                if c is not None:
                    act.wait_ge(s_xt, c + 1)
                    after(act, s_lg, c)
                    nc.scalar.copy(x1T[:, :], x1T_ps).then_inc(a_x1T, 1)
                if f is not None:
                    square(f, 1)
                if c is not None:
                    act.wait_ge(g_free, c + 1)
                    for k in range(2):
                        last = nc.scalar.copy(rows[:, par, k, :, 0:D], x1s[:, :, :])
                    last.then_inc(a_rows, 1)
                if f is not None:
                    act.wait_ge(s_vT, f + 1)
                    after(act, s_att, f)
                    nc.scalar.activation(vT[:, :], vT_ps, ACT.Identity, bias=bv_sb).then_inc(a_vT, 1)
                if f is not None:
                    act.wait_ge(s_stat, GB * f + GB)
                    nc.scalar.activation(lnss[:, :], ss_ps, ACT.Ln).then_inc(a_lnss, 1)
                if f is not None:
                    act.wait_ge(a_lnss, f + 1)
                    after(act, v_mm, f)
                    nc.scalar.activation(inv[:, :], lnss[:, :], ACT.Exp, scale=-0.5).then_inc(a_inv, 1)
                if f is not None:
                    act.wait_ge(s_kq, f + 1)
                    act.wait_ge(a_inv, f + 1)
                    after(act, v_gq, f)
                    after(act, s_den, f)
                    for q in range(GB):
                        last = nc.scalar.activation(g1[:, q, :], kq_ps[:, q, :], ACT.Copy, scale=invk[:, q:q + 1])
                    last.then_inc(a_g1, 1)
                if b is not None:
                    act.wait_ge(v_var, b + 1)
                    nc.scalar.activation(lnv[:, :], var[:, :], ACT.Ln).then_inc(a_lnv, 1)
                if b is not None:
                    act.wait_ge(a_lnv, b + 1)
                    after(act, v_rstd, b)
                    nc.scalar.activation(rstd0[:, :], lnv[:, :], ACT.Exp, scale=-0.5).then_inc(a_rstd, 1)
                if c is not None:
                    act.wait_ge(v_m2, c + 1)
                    after(act, v_p2, c)
                    nc.scalar.activation(ex[:, :, :], dl[:, :, :], ACT.Exp)
                    nc.scalar.activation(ex2[:, :], m2[:, :], ACT.Exp).then_inc(a_ex, 1)
                if b is not None:
                    act.wait_ge(v_nmr, b + 1)
                    after(act, s_xt, b)
                    after(act, a_rows, b)
                    after(act, s_keep, 16 * b)
                    for t in range(T - XV):
                        last = nc.scalar.activation(x1s[:, t, :], z[:, t, :], ACT.Identity,
                                                    bias=nmr[:, t:t + 1], scale=rstd[:, t:t + 1])
                    last.then_inc(a_x1, 1)
                if f is not None:
                    act.wait_ge(v_den, f + 1)
                    nc.scalar.activation(lnd[:, :, :], den[:, :, :], ACT.Ln, bias=width[:, 0:1]).then_inc(a_lnd, 1)
                    act.wait_ge(a_lnd, f + 1)
                    after(act, v_mm, f)
                    nc.scalar.activation(tail[:, :, :], lnd[:, :, :], ACT.Exp, scale=-1.0).then_inc(a_tail, 1)
                if more(f):
                    square(f + 1, 0)

            act.wait_ge(s_cols, 16)
            act.wait_ge(s_set, SET)
            act.preload_act_table_set(ACT_LN_EXP)
            square(0, 0)
            steps(act, step)
            act.preload_act_table_set(ACT_GELU)

            def tile_step(t, n, r):
                int_t = isinstance(t, int)
                if (not int_t or 1 <= t - 1 <= TILES):
                    act.wait_ge(p_y, t - 1)
                    after(act, p_yt, t - 2)
                    nc.scalar.activation(y_sb[:, :], y_ps, ACT.Identity, bias=bst[:, (r - 2) % RING, HC:HC + 1]
                                         ).then_inc(a_y, 1)
                if within(t):
                    act.wait_ge(s_bst[r], 16 * (n + 1))
                    for m in range(HC):
                        act.wait_ge(p_h, HC * t + m + 1)
                        after(act, v_hl, HC * (t - 1) + m + 1)
                        nc.scalar.activation(h_sb[:, m, :], h_ps[:, m, :], ACT.Gelu_apprx_tanh, bias=bst[:, r, m:m + 1]
                                             ).then_inc(a_h, 1)
                if (not int_t or 0 <= t - 2 < TILES):
                    act.wait_ge(p_yt, t - 1)
                    act.wait_ge(v_back, t - 1)
                    if not int_t:
                        act.wait_ge(s_ret[r % 4], 16 * SJ * n)
                    elif t >= 4:
                        act.wait_ge(s_ret[r % 4], 16 * SJ * (t // 4))
                    for j in range(SJ):
                        last = nc.scalar.activation(yo[:, r % 2, j, :], yt_ps[:, j * P:(j + 1) * P], ACT.Copy,
                                                    scale=back[:, (r - 2) % RING, j, 1:2])
                    last.then_inc(a_yo, 1)

            tiles(act, tile_step)
            act.preload_act_table_set(ACT_LN_EXP)
            for k in range(G // 2):
                act.wait_ge(f_var, k + 1)
                nc.scalar.activation(flnv[:, :], fvar[:, :], ACT.Ln).then_inc(g_lnv, 1)
                act.wait_ge(g_lnv, k + 1)
                after(act, f_rstd, k)
                nc.scalar.activation(frstd0[:, :], flnv[:, :], ACT.Exp, scale=-0.5).then_inc(g_rstd, 1)
                act.wait_ge(f_nmr, k + 1)
                for t in range(BT - vector_share(k)):
                    u = BT * k + t
                    last = nc.scalar.activation(x1_all[:, u, :], x1_all[:, u, :], ACT.Identity,
                                                bias=fnmr[:, t:t + 1], scale=frstd[:, t:t + 1])
                    if t in (T - 1, BT - vector_share(k) - 1):
                        last.then_inc(g_out, 1)

        @block.vector
        def _(ve):
            nc.vector.memset(ones[:, :], 1.0).then_inc(s_set, 1)
            nc.vector.memset(epsm[:, :], EPS_K).then_inc(s_set, 1)
            nc.vector.memset(ones16[:, :], 1.0).then_inc(s_set, 1)
            nc.vector.memset(width[:, :], float(D)).then_inc(s_set, 1)
            nc.vector.memset(pad_sb[:, :, :], 0.0).then_inc(v_pad, 1)
            ve.wait_ge(v_pad, 1)
            nc.vector.memset(pad_sb[:, :, D:D + 1].bitcast(I32), SKIP).then_inc(v_pad, 1)
            ve.wait_ge(s_vecs, 16)
            nc.vector.tensor_scalar(gam2[:, :], gam_sb, -0.5, None, ALU.mult).then_inc(s_set, 1)

            def biased_qk(g, b):
                ve.wait_ge(s_qk, GB * g + b + 1)
                after(ve, s_den, g)
                after(ve, a_sq, GB * g)
                nc.vector.tensor_tensor(
                    qk[:, 2 * b:2 * b + 2, :], qk_ps[:, b, :].rearrange("p (t n) -> p t n", t=2),
                    bqk_sb.unsqueeze(1).to_broadcast([P, 2, 2 * D]), ALU.add).then_inc(v_qk, 1)

            def wide(a):
                return a.unsqueeze(2).to_broadcast([P, T, E])

            def step(f, b, c, par):
                front, mid, rear = f is not None, b is not None, c is not None

                if mid:
                    ve.wait_ge(s_att, b + 1)
                    ve.wait_ge(s_x[1 - par], loaded(b, 1 - par))
                    after(ve, a_x1, b)
                    nc.vector.scalar_tensor_tensor(z[:, :, :].rearrange("p t d -> p (t d)"), att_ps, gam2[:, 0:1],
                                                   x_sb[:, 1 - par, :], ALU.mult, ALU.add).then_inc(v_z, 1)
                if rear:
                    ve.wait_ge(s_lg, c + 1)
                    nc.vector.tensor_reduce(m1[:, :], lg_ps[:, :, :], AX.X, ALU.max).then_inc(v_m1, 1)
                if mid:
                    ve.wait_ge(v_z, b + 1)
                    for t in range(T // 2):
                        nc.vector.bn_stats(st6[:, t, :], z[:, t, :])
                if rear:
                    ve.wait_ge(v_m1, c + 1)
                    after(ve, a_ex, c)
                    nc.vector.tensor_tensor(dl[:, :, :], lg_ps[:, :, :], wide(m1[:, :]), ALU.subtract).then_inc(v_dl, 1)
                if mid:
                    for t in range(T // 2, T):
                        last = nc.vector.bn_stats(st6[:, t, :], z[:, t, :])
                    last.then_inc(v_st, 1)
                if rear:
                    ve.wait_ge(v_dl, c + 1)
                    nc.vector.scalar_tensor_tensor(key1[:, :, :], dl[:, :, :], 0.0, rev, ALU.is_equal, ALU.mult
                                                   ).then_inc(v_key1, 1)
                    ve.wait_ge(g_free, c + 1)
                    src = ret_sb[:, c] if isinstance(c, int) else \
                        ret_sb[:, bass.ds(c, 1)].rearrange("p o k t -> p (o k) t")
                    nc.vector.tensor_copy(rows_i[:, par, :, :, D], src)
                    if mid:
                        ve.wait_ge(v_st, b + 1)
                    ve.wait_ge(v_key1, c + 1)
                    nc.vector.tensor_reduce(km1[:, :], key1[:, :, :], AX.X, ALU.max).then_inc(v_km1, 1)
                if mid:
                    if not rear:
                        ve.wait_ge(v_st, b + 1)
                    for t in range(T):
                        last = nc.vector.bn_aggr(mv[:, t, :], st6[:, t, :])
                    last.then_inc(v_mv, 1)
                if rear:
                    ve.wait_ge(v_km1, c + 1)
                    nc.vector.tensor_tensor(oh12[:, 0, :, :], rev, wide(km1[:, :]), ALU.is_equal).then_inc(v_oh1, 1)
                if mid:
                    ve.wait_ge(v_mv, b + 1)
                    nc.vector.tensor_scalar(var[:, :], mv[:, :, 1], EPS_LN / 4, None, ALU.add).then_inc(v_var, 1)
                if rear:
                    ve.wait_ge(v_oh1, c + 1)
                    nc.vector.scalar_tensor_tensor(dl2[:, :, :], oh12[:, 0, :, :], NEG, dl[:, :, :], ALU.mult, ALU.add
                                                   ).then_inc(v_dl2, 1)
                    ve.wait_ge(v_dl2, c + 1)
                    nc.vector.tensor_reduce(m2[:, :], dl2[:, :, :], AX.X, ALU.max).then_inc(v_m2, 1)
                    ve.wait_ge(v_m2, c + 1)
                    nc.vector.tensor_tensor(eq2[:, :, :], dl2[:, :, :], wide(m2[:, :]), ALU.is_equal).then_inc(v_eq2, 1)
                if front:
                    ve.wait_ge(a_g1, f + 1)
                    nc.vector.tensor_tensor(gq[:, :, :], g1[:, :, :], invq, ALU.mult).then_inc(v_gq, 1)
                if rear:
                    ve.wait_ge(v_eq2, c + 1)
                    nc.vector.tensor_tensor(key2[:, :, :], eq2[:, :, :], rev, ALU.mult).then_inc(v_key2, 1)
                if mid:
                    ve.wait_ge(a_rstd, b + 1)
                    ve.wait_ge(v_var, b + 1)
                    nc.vector.scalar_tensor_tensor(nwt[:, :], var[:, :], -0.5, rstd0[:, :], ALU.mult, ALU.mult
                                                   ).then_inc(v_nwt, 1)
                if rear:
                    ve.wait_ge(v_key2, c + 1)
                    nc.vector.tensor_reduce(km2[:, :], key2[:, :, :], AX.X, ALU.max).then_inc(v_km2, 1)
                if mid:
                    ve.wait_ge(v_nwt, b + 1)
                    nc.vector.tensor_tensor(nwt2[:, :], nwt[:, :], rstd0[:, :], ALU.mult).then_inc(v_nwt2, 1)
                if rear:
                    ve.wait_ge(v_km2, c + 1)
                    nc.vector.tensor_tensor(oh12[:, 1, :, :], rev, wide(km2[:, :]), ALU.is_equal).then_inc(v_oh2, 1)
                if mid:
                    ve.wait_ge(v_nwt2, b + 1)
                    nc.vector.scalar_tensor_tensor(rstd[:, :], nwt2[:, :], 1.5, rstd0[:, :], ALU.add, ALU.mult
                                                   ).then_inc(v_rstd, 1)
                if rear:
                    ve.wait_ge(v_oh2, c + 1)
                    after(ve, s_rk, c)
                    nc.vector.tensor_tensor(oh16[:, :, :], oh12[:, 0, :, :], oh12[:, 1, :, :], ALU.add).then_inc(v_oh, 1)
                if mid:
                    ve.wait_ge(v_rstd, b + 1)
                    nc.vector.scalar_tensor_tensor(nmr[:, :], mv[:, :, 0], -1.0, rstd[:, :], ALU.mult, ALU.mult
                                                   ).then_inc(v_nmr, 1)
                    ve.wait_ge(v_nmr, b + 1)
                    after(ve, s_xt, b)
                    after(ve, a_rows, b)
                    after(ve, s_keep, 16 * b)
                    for t in range(T - XV, T):
                        last = nc.vector.tensor_scalar(x1s[:, t, :], z[:, t, :], rstd[:, t:t + 1], nmr[:, t:t + 1],
                                                       ALU.mult, ALU.add)
                    last.then_inc(v_x1, 1)
                if front:
                    ve.wait_ge(s_den, f + 1)
                    after(ve, a_lnd, f)
                    nc.vector.tensor_tensor(den[:, :, :], kq_ps[:, :, :], invq, ALU.mult).then_inc(v_den, 1)
                if more(f):
                    biased_qk(f + 1, 0)
                if rear:
                    ve.wait_ge(s_rk, c + 1)
                    after(ve, v_base, c)
                    nc.vector.tensor_tensor(place[:, :, :], rk_ps[:, :, :],
                                            base[:, par, :].unsqueeze(1).to_broadcast([P, T, E]), ALU.add).then_inc(v_place, 1)
                    nc.vector.tensor_tensor(base[:, 1 - par, :], base[:, par, :], tot_ps, ALU.add).then_inc(v_base, 1)
                    ve.wait_ge(a_ex, c + 1)
                    nc.vector.tensor_reduce(zs[:, :], ex[:, :, :], AX.X, ALU.add).then_inc(v_zs, 1)
                    ve.wait_ge(v_place, c + 1)
                    nc.vector.tensor_tensor(sel_ke, oh12_ke, place_e.unsqueeze(1).to_broadcast([P, 2, T * E]), ALU.mult
                                            ).then_inc(v_sel, 1)
                    ve.wait_ge(v_zs, c + 1)
                    nc.vector.reciprocal(rz, zs[:, :]).then_inc(v_rz, 1)
                    ve.wait_ge(v_sel, c + 1)
                    with nc.allow_low_precision(reason="one whole number below 2^24, the rest zeros"):
                        nc.vector.tensor_reduce(pos[:, par, :, :], sel[:, :, :, :], AX.X, ALU.add)
                if front:
                    ve.wait_ge(a_tail, f + 1)
                    ve.wait_ge(v_den, f + 1)
                    nc.vector.scalar_tensor_tensor(ndr, den[:, :, :], float(D), tail[:, :, :],
                                                   ALU.add, ALU.mult).then_inc(v_ndr, 1)
                if rear:
                    ve.wait_ge(v_rz, c + 1)
                    nc.vector.tensor_tensor(p2, ex2[:, :], rz, ALU.mult).then_inc(v_p2, 1)
                if front:
                    ve.wait_ge(v_ndr, f + 1)
                    nc.vector.scalar_tensor_tensor(ntail[:, :, :], ndr, -2.0, tail[:, :, :],
                                                   ALU.add, ALU.mult).then_inc(v_tail, 1)
                if rear:
                    ve.wait_ge(v_p2, c + 1)
                    nc.vector.scalar_tensor_tensor(ps_[:, :], p2, 1e-8, rz, ALU.add, ALU.add).then_inc(v_ps, 1)
                if front:
                    ve.wait_ge(v_tail, f + 1)
                    ve.wait_ge(v_gq, f + 1)
                    after(ve, s_att, f)
                    nc.vector.scalar_tensor_tensor(mm[:, :, :], gq[:, :, :], 1.0, ntail[:, :, :],
                                                   ALU.add, ALU.mult).then_inc(v_mm, 1)
                if rear:
                    ve.wait_ge(v_ps, c + 1)
                    nc.vector.reciprocal(rs[:, :], ps_[:, :]).then_inc(v_rs, 1)
                if more(f):
                    biased_qk(f + 1, 1)
                if rear:
                    ve.wait_ge(v_rs, c + 1)
                    nc.vector.tensor_tensor(rows[:, par, :, :, D + 1], p12[:, :, :],
                                            rs[:, :].unsqueeze(1).to_broadcast([P, 2, T]), ALU.mult).then_inc(v_row, 1)
                    if isinstance(c, int) and c == 0:
                        ve.wait_ge(s_whi, 16)
                    ve.wait_ge(s_wraw[par], loaded(c, par))
                    low_half(c, wraw[:, par, :])
                if isinstance(f, int) and f == 0:
                    ve.wait_ge(s_const, CONST)
                    nc.vector.tensor_copy(tri16[:, :], k_sb[:, K_TRI:K_TRI + P]).then_inc(v_const, 1)
                    nc.vector.tensor_copy(base[:, 0, :], k_sb[:, K_BASE:K_BASE + E]).then_inc(v_const, 1)
                    ve.wait_ge(v_const, 2)

            wsp_n = wsp[:, :, :, :, :].rearrange("p e w a h -> p (e w) a h")

            def low_half(n, src):
                hi, lo = [wsp_n[:, n, a, :] if isinstance(n, int) else
                          wsp_n[:, bass.ds(n, 1), a, :].rearrange("p o h -> p (o h)") for a in range(2)]
                nc.vector.tensor_tensor(lo, src, hi.bitcast(F32), ALU.subtract).then_inc(s_wlo, 1)

            for b in range(GB):
                biased_qk(0, b)
            steps(ve, step)

            def chain(ins, n=[0]):
                ins.then_inc(v_chain, 1)
                n[0] += 1
                ve.wait_ge(v_chain, n[0])

            ve.wait_ge(v_base, G)
            nc.vector.tensor_copy(pad_i[:, :], base[:, G % 2, :]).then_inc(v_tab, 1)
            chain(nc.vector.tensor_tensor(cnt[:, :], base[:, G % 2, :], k_sb[:, K_BASE:K_BASE + E], ALU.subtract))
            chain(nc.vector.tensor_tensor(over[:, :, :], cnt[:, :].unsqueeze(2).to_broadcast([P, E, NF]), thr, ALU.is_gt))
            chain(nc.vector.tensor_reduce(ntile[:, :], over[:, :, :], AX.X, ALU.add))
            chain(nc.vector.tensor_tensor_scan(cum[:, :], ones[:, 0:E], ntile[:, :], 0.0, ALU.mult, ALU.add))
            chain(nc.vector.tensor_tensor(past[:, :, :], cum[:, :].unsqueeze(1).to_broadcast([P, TILES, E]), tno, ALU.is_le))
            chain(nc.vector.tensor_tensor(pastn[:, :, :], past[:, :, :],
                                          ntile[:, :].unsqueeze(1).to_broadcast([P, TILES, E]), ALU.mult))
            chain(nc.vector.tensor_reduce(tex[:, :], past[:, :, :], AX.X, ALU.add))
            chain(nc.vector.tensor_reduce(tst[:, :], pastn[:, :, :], AX.X, ALU.add))
            chain(nc.vector.scalar_tensor_tensor(toff[:, :], tst[:, :], -float(SLOTS), tsl, ALU.mult, ALU.add))
            chain(nc.vector.scalar_tensor_tensor(trow[:, :], tex[:, :], float(REG), toff[:, :], ALU.mult, ALU.add))
            nc.vector.tensor_scalar(row_i[:, :], trow[:, :], float(E * REG), None, ALU.min).then_inc(v_tab, 1)
            nc.vector.tensor_scalar(exp_i[:, :], tex[:, :], float(E - 1), None, ALU.min).then_inc(v_tab, 1)

            ve.wait_ge(s_raw, 32)
            for n in range(RAW_XG, RAW_END):
                low_half(n, raw_xg[:, n - RAW_XG, :] if n < RAW_YO else raw_yo[:, n - RAW_YO, :])
            for n in range(RAW_END, 2 * E):
                ve.wait_ge(s_wraw[n % 2], 16 * (E // 2 + 1))
                low_half(n, wraw[:, n % 2, :])

            def tile_step(t, n, r):
                par = r % 2
                int_t = isinstance(t, int)

                def halves(t):
                    ve.wait_ge(p_xg, t + 1)
                    after(ve, p_h, HC * t)
                    nc.vector.tensor_copy(xh[:, :], xg_ps).then_inc(v_xh, 1)
                    ve.wait_ge(v_xh, t + 1)
                    nc.vector.tensor_tensor(xl[:, :], xg_ps, xh[:, :].bitcast(F32), ALU.subtract).then_inc(v_xl, 1)

                if int_t and t == 0:
                    halves(0)
                if (not int_t or 1 <= t <= TILES):
                    ve.wait_ge(s_tile[(r - 1) % RING], 16 * ((t - 1) // RING + 1 if int_t else (n + (r > 0))))
                    if not int_t:
                        ve.wait_ge(s_ret[(r - 1) % RING], 16 * SJ * (n if r > 0 else n - 1))
                    elif t > RING:
                        ve.wait_ge(s_ret[(r - 1) % RING], 16 * SJ * ((t - 1) // RING))
                    nc.vector.tensor_copy(back[:, (r - 1) % RING, :, :].bitcast(I32), xg[:, (r - 1) % RING, :, D:D + 2].bitcast(I32)
                                          ).then_inc(v_back, 1)
                if within(t):
                    for m in range(HC):
                        ve.wait_ge(a_h, HC * t + m + 1)
                        after(ve, p_y, t - 1)
                        nc.vector.tensor_copy(hh[:, par, m, :], h_sb[:, m, :]).then_inc(v_hh, 1)
                        ve.wait_ge(v_hh, HC * t + m + 1)
                        nc.vector.tensor_tensor(hl[:, par, m, :], h_sb[:, m, :], hh[:, par, m, :].bitcast(F32),
                                                ALU.subtract).then_inc(v_hl, 1)
                        if m == 1 and (not int_t or t + 1 < TILES):
                            halves(t + 1)

            tiles(ve, tile_step)

            for c in range(G + 1):
                k = c // 2 - 1 if c % 2 == 0 and c > 0 else None
                if c < G:
                    xs = x1_all[:, T * c:T * (c + 1), :].rearrange("p t d -> p (t d)")
                    ve.wait_ge(g_z1, c + 1)
                    nc.vector.tensor_tensor(xs, xs, y1[c % YRING], ALU.add).then_inc(f_z, 1)
                if k is not None:
                    ve.wait_ge(g_rstd, k + 1)
                    nc.vector.scalar_tensor_tensor(fnwt[:, :], fvar[:, :], -0.5, frstd0[:, :], ALU.mult, ALU.mult
                                                   ).then_inc(f_nwt, 1)
                if c < G:
                    ve.wait_ge(f_z, c + 1)
                    for t in range(T // 2):
                        nc.vector.bn_stats(st6[:, t, :], x1_all[:, T * c + t, :])
                if k is not None:
                    ve.wait_ge(f_nwt, k + 1)
                    nc.vector.tensor_tensor(fnwt2[:, :], fnwt[:, :], frstd0[:, :], ALU.mult).then_inc(f_nwt2, 1)
                if c < G:
                    for t in range(T // 2, T):
                        last = nc.vector.bn_stats(st6[:, t, :], x1_all[:, T * c + t, :])
                    last.then_inc(f_st, 1)
                if k is not None:
                    ve.wait_ge(f_nwt2, k + 1)
                    after(ve, g_out, 2 * k)
                    nc.vector.scalar_tensor_tensor(frstd[:, :], fnwt2[:, :], 1.5, frstd0[:, :], ALU.add, ALU.mult
                                                   ).then_inc(f_rstd, 1)
                    ve.wait_ge(f_rstd, k + 1)
                    nc.vector.scalar_tensor_tensor(fnmr[:, :], fmv[:, k % 2, :, 0], -1.0, frstd[:, :],
                                                   ALU.mult, ALU.mult).then_inc(f_nmr, 1)
                if c < G:
                    ve.wait_ge(f_st, c + 1)
                    for t in range(T):
                        last = nc.vector.bn_aggr(fmv[:, c // 2 % 2, c % 2 * T + t, :], st6[:, t, :])
                    last.then_inc(f_mv, 1)
                if k is not None and vector_share(k):
                    ve.wait_ge(f_nmr, k + 1)
                    for t in range(BT - vector_share(k), BT):
                        u = BT * k + t
                        last = nc.vector.tensor_scalar(x1_all[:, u, :], x1_all[:, u, :], frstd[:, t:t + 1],
                                                       fnmr[:, t:t + 1], ALU.mult, ALU.add)
                    last.then_inc(f_out, 1)
                if c % 2:
                    ve.wait_ge(f_mv, c + 1)
                    nc.vector.tensor_scalar(fvar[:, :], fmv[:, c // 2 % 2, :, 1], EPS_LN, None, ALU.add
                                            ).then_inc(f_var, 1)

        @block.gpsimd
        def _(pool):
            def scatter(c, par):
                pool.wait_ge(a_rows, c + 1)
                pool.wait_ge(v_row, c + 1)
                pool.sem_inc(g_turn, 1)
                for k in range(2):
                    for t in range(T):
                        nc.gpsimd.indirect_dma_start(
                            regions, bass.IndirectOffsetOnAxis(ap=pos[:, par, k, t:t + 1], axis=0),
                            rows[:, par, k, t, :], None).then_inc(s_scat[par], 16)
                    if k == 0 and not (isinstance(c, int) and c == 0):
                        pool.wait_ge(s_scat[1 - par], loaded(c - 1, 1 - par) * 2 * T)
                        pool.sem_inc(g_free, 1)

            pool.sem_inc(g_free, 2)
            pool.wait_ge(s_x[1], 16)
            pool.dma_start(wsp[:, :, :, 0, :].rearrange("p e w h -> p (e w) h"),
                           wts.rearrange("p e w h -> p (e w) h")).then_inc(s_whi, 16)
            scatter(0, 0)
            with pool.Fori(1, G // 2) as i:
                scatter(2 * i - 1, 1)
                scatter(2 * i, 0)
            scatter(G - 1, 1)

            last_row = pool.to_reg(2 * TOK - 1)

            def tile_step(t, n, r):
                if not isinstance(t, int) or 0 <= t - 2 < TILES:
                    pool.wait_ge(a_yo, t - 1)
                    pool.sem_inc(g_turn, 1)
                    for j in range(SJ):
                        nc.gpsimd.indirect_dma_start(
                            returned, bass.IndirectOffsetOnAxis(ap=back[:, (r - 2) % RING, j, 0:1].bitcast(I32), axis=0),
                            yo[:, r % 2, j, :], None, bounds_check=last_row, oob_is_err=False
                        ).then_inc(s_ret[(r - 2) % RING], 16)

            tiles(pool, tile_step)
            for r in range(RING):
                pool.wait_ge(s_ret[r], 16 * SJ * len(range(r, TILES, RING)))
            for c in range(G):
                pool.wait_ge(s_y[c % YRING], 32 * (c // YRING + 1))
                nc.gpsimd.tensor_tensor(y1[c % YRING], y1[c % YRING], y2[c % YRING], ALU.add).then_inc(g_z1, 1)


def kernel(L0_attn_x, L0_attn_Wq, L0_attn_bq, L0_attn_Wk, L0_attn_bk, L0_attn_Wv, L0_attn_bv, L0_attn_gamma,
           L0_ffn_router_w, L0_ffn_w1, L0_ffn_b1, L0_ffn_w2, L0_ffn_b2):
    import concourse.bacc as _bacc
    from concourse.bass_utils import run_bass_kernel_spmd as _run

    x = np.ascontiguousarray(L0_attn_x).reshape(TOK, D)
    w1T = np.transpose(L0_ffn_w1, (0, 2, 1))
    w2T = np.transpose(np.reshape(L0_ffn_w2, (E, D, HC, P)), (0, 3, 2, 1)).reshape(E, P, H)
    b1c = np.transpose(np.reshape(L0_ffn_b1, (E, HC, P)), (2, 0, 1))
    b2c = np.transpose(L0_ffn_b2, (1, 0))[:, :, None]
    consts = np.zeros((P, K_COLS), np.float32)
    consts[:, K_ID:K_ID + P] = np.eye(P)
    consts[:, K_TRI:K_TRI + P] = np.triu(np.ones((P, P)), 1)
    consts[:, K_REV:K_REV + T * E] = np.tile(E - np.arange(E), T)
    consts[:, K_BASE:K_BASE + E] = REG * np.arange(E)
    consts[:, K_THR:K_T] = np.tile(SLOTS * np.arange(NF), E)
    consts[:, K_T:K_TS] = np.repeat(np.arange(TILES), E)
    consts[:, K_TS:K_COLS] = SLOTS * np.arange(TILES)
    returns = (np.arange(P)[:, None, None, None] + GC * np.arange(G)[None, :, None, None]
               + TOK * np.arange(2)[None, None, :, None] + P * np.arange(T)[None, None, None, :]).astype(np.int32)
    arrays = {
        "x": x,
        "xT": x.T,
        "cols": np.concatenate([np.transpose(L0_attn_Wq), np.transpose(L0_attn_Wk), np.transpose(L0_attn_Wv),
                                np.transpose(L0_ffn_router_w), np.reshape(L0_attn_bv, (D, 1))], axis=1),
        "vecs": np.concatenate([L0_attn_bq, L0_attn_bk, L0_attn_gamma]),
        "wts": np.stack([np.transpose(w1T, (1, 0, 2)), np.transpose(w2T, (1, 0, 2))], axis=2),
        "bcols": np.concatenate([b1c, b2c], axis=2),
        "consts": consts,
        "returns": returns,
    }
    arrays = {"in_" + k: np.ascontiguousarray(v) for k, v in arrays.items()}
    nc = _bacc.Bacc("TRN2", target_bir_lowering=False, num_devices=1)
    args = [nc.dram_tensor(k, v.shape, mybir.dt.from_np(v.dtype), kind="ExternalInput").ap() for k, v in arrays.items()]
    args.append(nc.dram_tensor("out_0", (TOK, D), F32, kind="ExternalOutput").ap())
    args.append(nc.dram_tensor("regions", ((E + 1) * REG, ROW), F32, kind="Internal").ap())
    args.append(nc.dram_tensor("returned", (2 * TOK, D), F32, kind="Internal").ap())
    moe_layer(nc, *args)
    r = _run(nc, [arrays], core_ids=[0])
    return r.results[0]["out_0"].reshape(B, C, D)
```
